# Optimizing a Trainium2 kernel written in Bass

```python
import numpy as np
import jax
import jax.numpy as jnp

def _softmax(x, axis=-1):
    return jax.nn.softmax(x, axis=axis)

def _gelu(x):
    return jax.nn.gelu(x, approximate=True)

def _silu(x):
    return jax.nn.silu(x)

def _sigmoid(x):
    return jax.nn.sigmoid(x)

def _layernorm(x, axis=-1, eps=1e-05):
    m = jnp.mean(x, axis=axis, keepdims=True)
    v = jnp.var(x, axis=axis, keepdims=True)
    return (x - m) / jnp.sqrt(v + eps)

def _scatter_add(tgt, idx, src, axis=0):
    return tgt.at[idx].add(src)

def _segment_sum(src, seg, n):
    return jax.ops.segment_sum(src, seg, n)
kernel_name = 'mk_xattn_ffn_d1_seqx_r8_0faba2'

def setup_inputs(seed: int=0):
    np.random.seed(seed)
    _w = jnp.asarray

    def _rec_inputs():
        import jax
        import jax.numpy as jnp
        _rk = jax.random.key(seed)
        x = -0.0003929 + 0.9999 * jax.random.normal(jax.random.fold_in(_rk, 1), (128, 64, 128), jnp.float32)
        _lenS = 64 - jax.random.randint(jax.random.fold_in(_rk, 7), (128,), 0, max(1, 64 // 4) + 1, jnp.int32)
        _lenS2 = 64 - jax.random.randint(jax.random.fold_in(_rk, 8), (128,), 0, max(1, 64 // 4) + 1, jnp.int32)
        _ctx_1024P = jax.random.normal(jax.random.fold_in(_rk, 11), (128, 16, 128), jnp.float32)
        _ctx_1024c = jax.random.dirichlet(jax.random.fold_in(_rk, 511), 0.3 * jnp.ones((16,), jnp.float32), (128, 64))
        _ctx_1024t = jnp.einsum('bsk,bkd->bsd', _ctx_1024c, _ctx_1024P)
        _ctx_1024t = _ctx_1024t * jax.lax.rsqrt(jnp.mean(jnp.square(_ctx_1024t)) + 1e-12) * 0.953939
        ctx_1024 = 2.81802e-05 + 1.00001 * (_ctx_1024t + 0.3 * jax.random.normal(jax.random.fold_in(_rk, 611), (128, 64, 128), jnp.float32))
        return (x, ctx_1024)
    x, ctx_1024 = _rec_inputs()

    def _L0_xattn_setup():
        import jax, jax.numpy as jnp
        import numpy as np
        B, T, D = (8, 256, 128)
        key = jax.random.key(seed)
        kq, kk, kv = jax.random.split(key, 3)
        return {'query': jax.random.normal(kq, (B, T, D), dtype=jnp.float32), 'key': jax.random.normal(kk, (B, T, D), dtype=jnp.float32), 'value': jax.random.normal(kv, (B, T, D), dtype=jnp.float32)}
    _L0_xattn_all = _L0_xattn_setup()
    _L0_xattn_in = {k: v for k, v in _L0_xattn_all.items() if k in ()}
    del _L0_xattn_all

    def _L0_ffn_setup():
        import jax, jax.numpy as jnp
        import numpy as np
        E = 8
        H = 128
        M = 256
        K = 2
        SE = 1
        BSZ, SEQ = (2, 128)
        W_SCALE = 0.02
        key = jax.random.key(seed)
        ks = jax.random.split(key, 9)
        return {'x': jax.random.normal(ks[0], (BSZ, SEQ, H), jnp.float32), 'gate_w': jax.random.normal(ks[1], (E, H), jnp.float32) * W_SCALE, 'beta': jnp.zeros((E,), jnp.float32), 'gate_proj_w': jax.random.normal(ks[2], (E, H, M), jnp.float32) * W_SCALE, 'up_proj_w': jax.random.normal(ks[3], (E, H, M), jnp.float32) * W_SCALE, 'down_proj_w': jax.random.normal(ks[4], (E, M, H), jnp.float32) * W_SCALE, 'shared_gate_w': jax.random.normal(ks[5], (SE, H, M), jnp.float32) * W_SCALE, 'shared_up_w': jax.random.normal(ks[6], (SE, H, M), jnp.float32) * W_SCALE, 'shared_down_w': jax.random.normal(ks[7], (SE, M, H), jnp.float32) * W_SCALE}
    _L0_ffn_all = _L0_ffn_setup()
    _L0_ffn_in = {k: v for k, v in _L0_ffn_all.items() if k in ('gate_w', 'beta', 'gate_proj_w', 'up_proj_w', 'down_proj_w', 'shared_gate_w', 'shared_up_w', 'shared_down_w')}
    del _L0_ffn_all
    return {'x': x, 'ctx_1024': ctx_1024, 'L0_ffn_gate_w': _L0_ffn_in['gate_w'], 'L0_ffn_beta': _L0_ffn_in['beta'], 'L0_ffn_gate_proj_w': _L0_ffn_in['gate_proj_w'], 'L0_ffn_up_proj_w': _L0_ffn_in['up_proj_w'], 'L0_ffn_down_proj_w': _L0_ffn_in['down_proj_w'], 'L0_ffn_shared_gate_w': _L0_ffn_in['shared_gate_w'], 'L0_ffn_shared_up_w': _L0_ffn_in['shared_up_w'], 'L0_ffn_shared_down_w': _L0_ffn_in['shared_down_w']}

def reference(x, ctx_1024, L0_ffn_gate_w, L0_ffn_beta, L0_ffn_gate_proj_w, L0_ffn_up_proj_w, L0_ffn_down_proj_w, L0_ffn_shared_gate_w, L0_ffn_shared_up_w, L0_ffn_shared_down_w):
    import jax
    import jax.numpy as jnp

    def _L0_xattn_ref(query, key, value):
        import jax, jax.numpy as jnp
        import numpy as np
        B, T, D = (8, 256, 128)
        d = query.shape[-1]
        scores = jnp.einsum('bqd,bkd->bqk', query, key) * d ** (-0.5)
        tril = jnp.tril(jnp.ones((query.shape[1], key.shape[1]), dtype=bool))
        scores = jnp.where(tril, scores, -jnp.inf)
        attn = jax.nn.softmax(scores, axis=-1)
        return jnp.einsum('bqk,bkd->bqd', attn, value)

    def _L0_ffn_ref(x, gate_w, beta, gate_proj_w, up_proj_w, down_proj_w, shared_gate_w, shared_up_w, shared_down_w):
        import jax, jax.numpy as jnp
        import numpy as np
        E = 8
        H = 128
        M = 256
        K = 2
        SE = 1
        BSZ, SEQ = (2, 128)
        W_SCALE = 0.02
        B0, S0, H0 = x.shape
        xt = x.reshape(-1, H0)
        B = xt.shape[0]
        logits = xt @ gate_w.T
        _, idx = jax.lax.top_k(logits + beta, K)
        probs = jax.nn.sigmoid(jnp.take_along_axis(logits, idx, axis=-1))
        c = jnp.zeros((B, E), xt.dtype).at[jnp.arange(B)[:, None], idx].add(probs)
        g = jnp.einsum('bh,ehm->bem', xt, gate_proj_w)
        u = jnp.einsum('bh,ehm->bem', xt, up_proj_w)
        h = jax.nn.silu(g) * u
        eo = jnp.einsum('bem,emh->beh', h, down_proj_w)
        combined = jnp.einsum('beh,be->bh', eo, c)
        sg = jnp.einsum('bh,ehm->bem', xt, shared_gate_w)
        su = jnp.einsum('bh,ehm->bem', xt, shared_up_w)
        sh = jax.nn.silu(sg) * su
        shared_out = jnp.einsum('bem,emh->beh', sh, shared_down_w).sum(axis=1)
        return (combined + shared_out).reshape(B0, S0, H0)
    x = x + _L0_xattn_ref(_layernorm(x, axis=-1), ctx_1024, ctx_1024)
    x = x + _L0_ffn_ref(_layernorm(x, axis=-1), L0_ffn_gate_w, L0_ffn_beta, L0_ffn_gate_proj_w, L0_ffn_up_proj_w, L0_ffn_down_proj_w, L0_ffn_shared_gate_w, L0_ffn_shared_up_w, L0_ffn_shared_down_w)
    return x

_drawn_inputs = setup_inputs


def setup_inputs(seed=0):
    import zlib

    import numpy as np

    out = dict(_drawn_inputs(seed))
    spreads = {'L0_ffn_beta': (0.0, 0.8)}
    factors = {'L0_ffn_gate_w': 8.0,
     'L0_ffn_gate_proj_w': 8.0,
     'L0_ffn_up_proj_w': 8.0,
     'L0_ffn_down_proj_w': 8.0,
     'L0_ffn_shared_gate_w': 8.0,
     'L0_ffn_shared_up_w': 8.0,
     'L0_ffn_shared_down_w': 8.0}
    for name, (base, spread) in spreads.items():
        noise = np.random.default_rng([zlib.crc32(name.encode()), seed]).standard_normal(out[name].shape)
        drawn = base * np.exp(spread * noise) if base else spread * noise
        out[name] = jnp.asarray(drawn.astype(out[name].dtype))
    for name, factor in factors.items():
        out[name] = (out[name] * factor).astype(out[name].dtype)
    return out
```

```python
from contextlib import ExitStack

import concourse.bass as bass
from concourse import mybir

F32 = mybir.dt.float32
F32R = mybir.dt.float32r
BF16 = mybir.dt.bfloat16
U32 = mybir.dt.uint32
ALU = mybir.AluOpType
ACT = mybir.ActivationFunctionType
AX_X = mybir.AxisListType.X

P = 128
EPS = 1e-5
MASKED = -1e30


class Program:

    def __init__(self, nc, ctx):
        self.nc, self.ctx = nc, ctx
        self.queues = {"pe": [], "act": [], "dve": [], "pool": [], "sp": []}
        self.sems, self.counts = {}, {}
        self.waited = {}

    def do(self, engine, waits, issue, signal, by=1):
        if signal not in self.sems:
            self.sems[signal] = self.ctx.enter_context(self.nc.semaphore("s_" + signal))
            self.counts[signal] = 0
        self.counts[signal] += by
        for token in waits:
            if token is not None and self.waited.get((engine, token[0]), 0) < token[1]:
                self.waited[engine, token[0]] = token[1]
                self.queues[engine].append(lambda e, t=token: e.wait_ge(self.sems[t[0]], t[1]))
        self.queues[engine].append(lambda e: issue(e).then_inc(self.sems[signal], by))
        return signal, self.counts[signal]

    def load(self, engine, waits, out, in_, signal):
        return self.do(engine, waits, lambda e: e.dma_start(out, in_), signal, 16)

    def run(self, engine, e):
        for issue in self.queues[engine]:
            issue(e)


def build(nc, x, ctx_in, gate_w, beta, gate_proj, up_proj, down_proj, shared_gate, shared_up,
          shared_down, out):
    B, T, D = x.shape
    E, _, M = gate_proj.shape
    MC = M // P
    NE = E + 1
    NB = 2 * 4
    GT = 4
    GN = GT * P
    G = B * T // GN
    SCALE = float(D) ** -0.5
    assert T == 64 and D == P and M == 2 * P

    x_rows = x.rearrange("b s d -> (b s) d").rearrange("(g t p) d -> g p t d", g=G, t=GT)
    out_rows = out.rearrange("b s d -> (b s) d").rearrange("(g t p) d -> g p t d", g=G, t=GT)
    ctx_rows = ctx_in.rearrange("(g b) s d -> g s b d", g=G)

    with ExitStack() as ctx:
        prog = Program(nc, ctx)
        do, load = prog.do, prog.load

        def sb(name, shape, dt=F32):
            return ctx.enter_context(nc.sbuf_tensor(name, shape, dt))

        def bank(name):
            return ctx.enter_context(nc.psum_tensor(name, [P, 512], F32))

        ident = sb("ident", [P, P])
        ident_bf = sb("ident_bf", [P, P], BF16)
        mask = sb("mask", [P, GT, T], BF16)
        minus_half = sb("minus_half", [P, GT])
        expert_number = sb("expert_number", [P, GT, E])
        beta_all = sb("beta_all", [P, E])
        w_gu = sb("w_gu", [P, NE, 2, M])
        w_gu_hi = sb("w_gu_hi", [P, NE, 2, M], F32R)
        w_gu_lo = sb("w_gu_lo", [P, NE, 2, M], F32R)
        w_dn = sb("w_dn", [P, NE, MC, D])
        w_dn_hi = sb("w_dn_hi", [P, NE, MC, D], F32R)
        w_dn_lo = sb("w_dn_lo", [P, NE, MC, D], F32R)
        router = sb("router", [E, D])
        router_T = sb("router_T", [D, E])
        x_sb = sb("x_sb", [P, 2, GT, D])
        c_sb = sb("c_sb", [T, 2, NB, D])
        stats = sb("stats", [P, GT, 6])
        moments = sb("moments", [P, GT, 2])
        var_eps = sb("var_eps", [P, GT])
        rstd = sb("rstd", [P, GT])
        xn = sb("xn", [P, GT, D])
        xn_T = sb("xn_T", [D, GN])
        ctx_T = sb("ctx_T", [D, NB, T])
        neg_max = sb("neg_max", [P, GT])
        exp_bias = sb("exp_bias", [P, GT])
        probs = sb("probs", [P, GT, T])
        row_sum = sb("row_sum", [P, GT])
        inv_sum = sb("inv_sum", [P, GT])
        probs_T = sb("probs_T", [T, GN])
        x2 = sb("x2", [P, 2, GT, D])
        xn2_T = sb("xn2_T", [D, GN])
        xn2_hi = sb("xn2_hi", [D, 2, GN], F32R)
        xn2_lo = sb("xn2_lo", [D, 2, GN], F32R)
        logits = sb("logits", [P, GT, E])
        biased = sb("biased", [P, GT, E])
        top8 = sb("top8", [P, GT, 8])
        top_index = sb("top_index", [P, GT, 8], U32)
        top_index_f = sb("top_index_f", [P, GT, 8])
        chosen = sb("chosen", [P, 2, GT, E])
        sig = sb("sig", [P, 3, GT, E])
        weight = sb("weight", [P, 2, GT, E])
        silu = sb("silu", [P, MC, GN])
        hid = sb("hid", [P, MC, GN])
        hid_hi = sb("hid_hi", [P, 2, MC, GN], F32R)
        hid_lo = sb("hid_lo", [P, 2, MC, GN], F32R)
        acc = sb("acc", [P, 2, GT, D])

        att = [bank("att0"), bank("att1")]
        gu_bank = [[bank(f"gu{m}{i}") for i in range(2)] for m in range(MC)]
        y_bank = [bank("y0"), bank("y1")]

        t = do("pool", [], lambda e: e.memset(ident[:], 0.0), "const")
        t = do("pool", [t], lambda e: e.affine_select(
            out=ident[:], in_=ident[:], compare_op=ALU.not_equal, fill=1.0, base=0,
            pattern=[[-1, P]], channel_multiplier=1), "const")
        t = do("pool", [t], lambda e: e.tensor_copy(ident_bf[:], ident[:]), "const")
        t = do("pool", [t], lambda e: e.memset(mask[:], 0.0), "const")
        for half in range(2):
            part = mask[half * T:(half + 1) * T]
            t = do("pool", [t], lambda e, part=part: e.affine_select(
                out=part, in_=part, compare_op=ALU.is_ge, fill=MASKED, base=0,
                pattern=[[0, GT], [-1, T]], channel_multiplier=1), "const")
        t = do("pool", [t], lambda e: e.memset(minus_half[:], -0.5), "const")
        constants = do("pool", [t], lambda e: e.iota(
            expert_number[:], pattern=[[0, GT], [1, E]], base=0, channel_multiplier=0,
            allow_small_or_imprecise_dtypes=True), "const")

        def load_group(g):
            buf = g % 2
            free = [x2_done[g - 2]] if g >= 2 else []
            a = load("sp", free, x_sb[:, buf], x_rows[g], f"x_in{buf}")
            b = load("sp", [attended[g - 2], ctx_T_done[g - 2]] if g >= 2 else [],
                     c_sb[:, buf], ctx_rows[g], f"c_in{buf}")
            return a, b

        loaded, x2_done, attended, ctx_T_done = {}, {}, {}, {}
        loaded[0] = load_group(0)
        small_in = load("sp", [], router[:], gate_w, "router_in")
        beta_in = load("sp", [], beta_all[:], beta.rearrange("(a e) -> a e", a=1).broadcast_to([P, E]), "beta_in")
        load("act", [], w_gu[:, 0, 0], shared_gate[0], "w_in0")
        load("act", [], w_gu[:, 0, 1], shared_up[0], "w_in0")
        w_in = {0: load("act", [], w_dn[:, 0], shared_down[0].rearrange("(c p) h -> p c h", c=MC), "w_in0")}
        loaded[1] = load_group(1)
        for ex in range(E):
            load("act", [], w_gu[:, ex + 1, 0], gate_proj[ex], f"w_in{ex + 1}")
            load("act", [], w_gu[:, ex + 1, 1], up_proj[ex], f"w_in{ex + 1}")
            w_in[ex + 1] = load("act", [], w_dn[:, ex + 1],
                                down_proj[ex].rearrange("(c p) h -> p c h", c=MC), f"w_in{ex + 1}")

        def split_weights(n):
            def hi(e):
                e.tensor_copy(w_gu_hi[:, n], w_gu[:, n])
                return e.tensor_copy(w_dn_hi[:, n], w_dn[:, n])
            h = do("dve", [w_in[n]], hi, "w_hi")

            def lo(e):
                e.tensor_tensor(w_gu_lo[:, n], w_gu[:, n], w_gu_hi[:, n].bitcast(F32), ALU.subtract)
                return e.tensor_tensor(w_dn_lo[:, n], w_dn[:, n], w_dn_hi[:, n].bitcast(F32), ALU.subtract)
            return do("pool", [h], lo, "w_lo")

        r = do("pe", [small_in, constants], lambda e: e.transpose(att[0][:, 0:E], router[:], ident[0:E, 0:E]), "router_T")
        router_done = do("dve", [r], lambda e: e.tensor_copy(router_T[:], att[0][:, 0:E]), "router_T_copy")

        last = {k: None for k in ("xn_T", "ctx_T", "scores", "exp", "pT", "probs_T", "o", "x2", "xn2_T",
                                  "split", "logits", "routed", "a_free0", "a_free1", "bias", "norm1", "norm2",
                                  "transposed1", "transposed2", "logit_mm", "sum", "exp_l", "idx")}
        last["a_free0"] = router_done
        h_free = {}

        def normalise(g, src, waits, out_wait, signal):
            def st(e):
                for i in range(GT):
                    r = e.bn_stats(stats[:, i], src[:, i])
                return r
            a = do("dve", waits, st, "stats")

            def ag(e):
                for i in range(GT):
                    r = e.bn_aggr(moments[:, i], stats[:, i])
                return r
            b = do("dve", [a, out_wait], ag, "moments")
            c = do("pool", [b], lambda e: e.tensor_scalar(var_eps[:], moments[:, :, 1], EPS, None, ALU.add), "var_eps")
            c = do("pool", [c], lambda e: e.tensor_tensor(rstd[:], var_eps[:], minus_half[:], ALU.pow), "rstd")

            def nm(e):
                for i in range(GT):
                    r = e.tensor_scalar(xn[:, i], src[:, i], moments[:, i, 0:1], rstd[:, i:i + 1],
                                        ALU.subtract, ALU.mult)
                return r
            return do("dve", [c], nm, signal)

        def attention_steps(g):
            buf = g % 2
            A, Bk = att
            x_in, c_in = loaded[g]
            last["norm1"] = normalise(g, x_sb[:, buf], [x_in], last["transposed2"], "norm1")

            def tc(e):
                for b in range(NB):
                    r = e.transpose(Bk[:, b * T:(b + 1) * T], c_sb[:, buf, b], ident[0:T, 0:T])
                return r
            t = do("pe", [c_in, constants, last["a_free1"]], tc, "ctx_transposed")
            ctx_T_done[g] = t
            last["ctx_T"] = do("act", [t, last["scores"]], lambda e: e.activation(
                ctx_T[:, :, :], Bk[:, :].rearrange("p (b s) -> p b s", b=NB), ACT.Copy), "ctx_T")
            yield

            def tx(e):
                for i in range(GT):
                    r = e.transpose(A[:, i * P:(i + 1) * P], xn[:, i], ident[:])
                return r
            last["transposed1"] = do("pe", [last["norm1"], constants, last["a_free0"]], tx, "xn_transposed")
            last["xn_T"] = do("act", [last["transposed1"], last["scores"]],
                              lambda e: e.activation(xn_T[:], A[:], ACT.Copy), "xn_T")
            yield

            def sc(e):
                e.matmul(A[:, 0:GT * T], ident_bf[:], mask[:, :, :].rearrange("p t k -> p (t k)"),
                         start=True, stop=False, skip_group_check=True)
                for i in range(GT):
                    for half in range(2):
                        q = xn_T[:, i * P + half * T:i * P + (half + 1) * T]
                        r = e.matmul(A[half * T:(half + 1) * T, i * T:(i + 1) * T], q, ctx_T[:, 2 * i + half],
                                     start=False, stop=True, skip_group_check=True)
                return r
            last["scores"] = do("pe", [last["xn_T"], last["ctx_T"]], sc, "scores")
            S = A[:, 0:GT * T].rearrange("p (t k) -> p t k", t=GT)
            mx = do("dve", [last["scores"], last["exp"]],
                    lambda e: e.tensor_reduce(neg_max[:], S, AX_X, ALU.max, negate=True), "row_max")
            last["bias"] = do("dve", [mx], lambda e: e.tensor_scalar(exp_bias[:], neg_max[:], SCALE, None, ALU.mult),
                              "exp_bias")

            def ex(e):
                for i in range(GT):
                    r = e.activation(probs[:, i], S[:, i], ACT.Exp, bias=exp_bias[:, i:i + 1], scale=SCALE,
                                     accum_out=row_sum[:, i:i + 1])
                return r
            last["exp"] = do("act", [last["bias"], last["pT"], last["sum"]], ex, "exp")
            yield

            def tp(e):
                for i in range(GT):
                    r = e.transpose(Bk[0:T, i * P:(i + 1) * P], probs[:, i], ident[:])
                return r
            last["pT"] = do("pe", [last["exp"], last["ctx_T"]], tp, "probs_transposed")
            last["probs_T"] = do("act", [last["pT"], last["o"]], lambda e: e.activation(probs_T[:], Bk[0:T, :], ACT.Copy),
                                 "probs_T")
            last["sum"] = do("dve", [last["exp"]], lambda e: e.reciprocal(inv_sum[:], row_sum[:]), "inv_sum")
            yield

            def pv(e):
                for i in range(GT):
                    for half in range(2):
                        r = e.matmul(A[half * T:(half + 1) * T, i * D:(i + 1) * D],
                                     probs_T[:, i * P + half * T:i * P + (half + 1) * T],
                                     c_sb[:, buf, 2 * i + half], start=True, stop=True, skip_group_check=True)
                return r
            last["o"] = attended[g] = do("pe", [last["probs_T"]], pv, "attended")

            def rs(e):
                for i in range(GT):
                    r = e.scalar_tensor_tensor(out=x2[:, buf, i], in0=A[:, i * D:(i + 1) * D], scalar=inv_sum[:, i:i + 1],
                                               in1=x_sb[:, buf, i], op0=ALU.mult, op1=ALU.add)
                return r
            x2_done[g] = do("dve", [last["o"], last["sum"], first_sum.get(g - 2)], rs, "x2")
            last["norm2"] = normalise(g, x2[:, buf], [x2_done[g]], last["transposed1"], "norm2")
            if g + 2 < G:
                loaded[g + 2] = load_group(g + 2)
            yield

            def tx2(e):
                for i in range(GT):
                    r = e.transpose(Bk[:, i * P:(i + 1) * P], xn[:, i], ident[:])
                return r
            last["transposed2"] = do("pe", [last["norm2"], last["probs_T"]], tx2, "xn2_transposed")
            full = do("act", [last["transposed2"], last["logit_mm"]],
                      lambda e: e.activation(xn2_T[:], Bk[:], ACT.Copy), "xn2_T")
            hi = do("dve", [last["transposed2"], full, gu_done.get((g - 2, NE - 1))],
                    lambda e: e.tensor_copy(xn2_hi[:, buf], Bk[:]), "xn2_hi")
            last["split"] = last["a_free1"] = do("dve", [hi], lambda e: e.tensor_tensor(
                xn2_lo[:, buf], Bk[:], xn2_hi[:, buf].bitcast(F32), ALU.subtract), "xn2_lo")
            yield

            def lg(e):
                for i in range(GT):
                    r = e.matmul(A[:, i * E:(i + 1) * E], xn2_T[:, i * P:(i + 1) * P], router_T[:], start=True, stop=True)
                return r
            last["logit_mm"] = do("pe", [full, router_done, x2_done[g]], lg, "logits_mm")
            L = A[:, 0:GT * E].rearrange("p (t e) -> p t e", t=GT)
            a = last["a_free0"] = do("dve", [last["logit_mm"], last["exp_l"]], lambda e: e.tensor_copy(logits[:, :, :], L), "logits")
            b = do("dve", [a, beta_in], lambda e: e.tensor_tensor(
                biased[:, :, :], logits[:, :, :], beta_all[:, :].rearrange("p (a e) -> p a e", a=1).broadcast_to([P, GT, E]), ALU.add), "biased")

            def mx8(e):
                for i in range(GT):
                    r = e.max(top8[:, i], biased[:, i])
                return r
            b = do("dve", [b], mx8, "top8")

            def mi(e):
                for i in range(GT):
                    r = e.max_index(top_index[:, i], top8[:, i], biased[:, i])
                return r
            b = do("dve", [b], mi, "top_index")
            b = do("dve", [b], lambda e: e.tensor_copy(top_index_f[:, :, :], top_index[:, :, :]), "top_index_f")

            def oh(e):
                for k in range(2):
                    r = e.tensor_tensor(chosen[:, k], expert_number[:, :, :],
                                        top_index_f[:, :, k:k + 1].broadcast_to([P, GT, E]), ALU.is_equal)
                return r
            b = do("dve", [b, constants], oh, "one_hot")
            b = do("dve", [b], lambda e: e.tensor_tensor(chosen[:, 0], chosen[:, 0], chosen[:, 1], ALU.add), "chosen")
            s = last["exp_l"] = do("act", [a, last["idx"]], lambda e: e.activation(sig[:, 0], logits[:, :, :], ACT.Exp, scale=-1.0), "exp_logits")
            s = do("dve", [s], lambda e: e.tensor_scalar(sig[:, 1], sig[:, 0], 1.0, None, ALU.add), "sig_sum")
            s = do("dve", [s], lambda e: e.reciprocal(sig[:, 2], sig[:, 1]), "sigmoid")
            last["idx"] = routed[g] = do("dve", [b, s, weighted.get((g - 2, NE - 1))], lambda e: e.tensor_tensor(
                weight[:, buf], chosen[:, 0], sig[:, 2], ALU.mult), "routed")
            yield

        gu_done, activated, split_done, weighted, first_sum, routed, stored = {}, {}, {}, {}, {}, {}, {}
        units = [(g, n) for g in range(G) for n in range(NE)]

        def gate_up(i):
            g, n = units[i]
            buf = g % 2
            before = units[i - 1] if i else None
            for m in range(MC):
                def mm(e, m=m):
                    for k in range(2):
                        w = [w_gu_hi[:, n, k, m * P:(m + 1) * P], w_gu_lo[:, n, k, m * P:(m + 1) * P]]
                        parts = [(w[0], xn2_hi), (w[0], xn2_lo), (w[1], xn2_hi)]
                        for j, (lhs, rhs) in enumerate(parts):
                            r = e.matmul(gu_bank[m][k][:], lhs, rhs[:, buf], start=(j == 0), stop=(j == 2))
                    return r
                mmd = do("pe", [xn2_ready[g], w_ready[n], activated.get((before, m))], mm, f"gate_up{m}")
                gu_done[g, n] = mmd
                a = do("act", [mmd, activated.get((before, m))],
                       lambda e, m=m: e.activation(silu[:, m], gu_bank[m][0][:], ACT.Silu), f"silu{m}")
                a = do("dve", [a, split_done.get((before, m))],
                       lambda e, m=m: e.tensor_tensor(hid[:, m], silu[:, m], gu_bank[m][1][:], ALU.mult), f"hid{m}")
                activated[(g, n), m] = a
                a = do("act", [a, down_done.get(i - 2)],
                       lambda e, m=m: e.activation(hid_hi[:, i % 2, m], hid[:, m], ACT.Copy), f"hid_hi{m}")
                split_done[(g, n), m] = do("pool", [a, down_done.get(i - 2)], lambda e, m=m: e.tensor_tensor(
                    hid_lo[:, i % 2, m], hid[:, m], hid_hi[:, i % 2, m].bitcast(F32), ALU.subtract), f"hid_lo{m}")

        down_done = {}

        def down(i):
            g, n = units[i]
            buf = g % 2

            def mm(e):
                for t in range(GT):
                    dst = y_bank[i % 2][:, t * D:(t + 1) * D]
                    j = 0
                    for m in range(MC):
                        h = [v[:, i % 2, m, t * P:(t + 1) * P] for v in (hid_hi, hid_lo)]
                        for lhs, rhs in ((h[0], w_dn_hi), (h[0], w_dn_lo), (h[1], w_dn_hi)):
                            r = e.matmul(dst, lhs, rhs[:, n, m], start=(j == 0), stop=(j == 3 * MC - 1))
                            j += 1
                return r
            d = down_done[i] = do("pe", [split_done[(g, n), 0], split_done[(g, n), 1],
                                         weighted.get(units[i - 2]) if i >= 2 else None], mm, "down")

            def ad(e):
                if n == 0:
                    return e.tensor_tensor(acc[:, buf], y_bank[i % 2][:, :].rearrange("p (t d) -> p t d", t=GT),
                                           x2[:, buf], ALU.add)
                for t in range(GT):
                    r = e.scalar_tensor_tensor(out=acc[:, buf, t], in0=y_bank[i % 2][:, t * D:(t + 1) * D],
                                               scalar=weight[:, buf, t, n - 1:n], in1=acc[:, buf, t],
                                               op0=ALU.mult, op1=ALU.add)
                return r
            w = [d, routed[g], weighted.get((g, n - 1)), stored.get(g - 2) if n == 0 else None]
            weighted[g, n] = do("dve", w, ad, "weighted")
            if n == 0:
                first_sum[g] = weighted[g, n]
            if n == NE - 1:
                stored[g] = load("sp", [weighted[g, n]], out_rows[g], acc[:, buf], f"store{buf}")

        w_ready, xn2_ready = {}, {}
        w_ready[0] = split_weights(0)
        for _ in attention_steps(0):
            pass
        xn2_ready[0] = last["split"]
        for i, (g, n) in enumerate(units):
            if n == 0 and g + 1 < G:
                steps = attention_steps(g + 1)
            if g == 0 and n + 1 < NE:
                w_ready[n + 1] = split_weights(n + 1)
            gate_up(i)
            if g + 1 < G:
                next(steps, None)
                if n == 5:
                    xn2_ready[g + 1] = last["split"]
            if i >= 1:
                down(i - 1)
        down(len(units) - 1)
        for g in (G - 2, G - 1):
            prog.queues["sp"].append(lambda e, t=stored[g]: e.wait_ge(prog.sems[t[0]], t[1]))

        block = ctx.enter_context(nc.Block())

        @block.sync
        def _(e):
            prog.run("sp", e)

        @block.gpsimd
        def _(e):
            prog.run("pool", e)

        @block.scalar
        def _(e):
            prog.run("act", e)

        @block.vector
        def _(e):
            prog.run("dve", e)

        @block.tensor
        def _(e):
            prog.run("pe", e)


_INS = ["x", "ctx_1024", "L0_ffn_gate_w", "L0_ffn_beta", "L0_ffn_gate_proj_w", "L0_ffn_up_proj_w", "L0_ffn_down_proj_w",
        "L0_ffn_shared_gate_w", "L0_ffn_shared_up_w", "L0_ffn_shared_down_w"]


def kernel(**inputs):
    import numpy as np
    import concourse.bacc as bacc
    from concourse.bass_utils import run_bass_kernel_spmd

    nc = bacc.Bacc("TRN2", target_bir_lowering=False, num_devices=1)
    arrays, args = {}, []
    for name in _INS:
        a = np.ascontiguousarray(inputs[name])
        arrays[name] = a
        args.append(nc.dram_tensor(name, a.shape, mybir.dt.from_np(a.dtype), kind="ExternalInput").ap())
    shape = inputs["x"].shape
    args.append(nc.dram_tensor("out", shape, F32, kind="ExternalOutput").ap())
    build(nc, *args)
    return run_bass_kernel_spmd(nc, [arrays], core_ids=[0]).results[0]["out"]
```

```python
from contextlib import ExitStack

import concourse.bass as bass
from concourse import mybir

F32 = mybir.dt.float32
F32R = mybir.dt.float32r
BF16 = mybir.dt.bfloat16
U32 = mybir.dt.uint32
I32 = mybir.dt.int32
ALU = mybir.AluOpType
ACT = mybir.ActivationFunctionType
AX_X = mybir.AxisListType.X

P = 128
EPS = 1e-5
MASKED = -1e30


class Step:
    def __init__(self, engine, waits, issue, signal, by, ns, after, number):
        self.engine, self.issue, self.completion, self.by = engine, issue, signal, by
        self.waits = [t for t in waits if t is not None]
        self.ns, self.after, self.number = ns, after, number


class Program:
    LATENCY = 150
    DMA_LATENCY = 2200

    def __init__(self, nc, ctx):
        self.nc, self.ctx = nc, ctx
        self.steps = []
        self.order = {"pe": [], "act": [], "dve": [], "pool": [], "sp": []}
        self.sems, self.counts = {}, {}
        self.at_end = []

    def do(self, engine, waits, issue, signal, by=1, ns=100, after=None, late=0):
        if signal not in self.sems:
            self.sems[signal] = self.ctx.enter_context(self.nc.semaphore("s_" + signal))
            self.counts[signal] = 0
        self.counts[signal] += by
        self.steps.append(Step(engine, waits, issue, (signal, self.counts[signal]), by, ns, after,
                               len(self.steps) + late))
        return signal, self.counts[signal]

    def load(self, engine, waits, out, in_, signal):
        return self.do(engine, waits, lambda e: e.dma_start(out, in_), signal, 16, 60)

    def arrange(self):
        free = {name: 0 for name in self.order}
        known = {}
        waiting = {name: [] for name in self.order}
        for s in self.steps:
            waiting[s.engine].append(s)
        left = len(self.steps)
        while left:
            best = None
            for name, steps in waiting.items():
                seen = set()
                for s in steps[:160]:
                    if s.completion[0] in seen:
                        continue
                    seen.add(s.completion[0])
                    if any(t not in known for t in s.waits):
                        continue
                    start = max([free[name]] + [known[t] for t in s.waits])
                    if best is None or (start, s.number) < best[:2]:
                        best = (start, s.number, s)
            start, _, s = best
            free[s.engine] = start + s.ns
            known[s.completion] = start + s.ns + (self.DMA_LATENCY if s.by == 16 else self.LATENCY)
            waiting[s.engine].remove(s)
            self.order[s.engine].append(s)
            left -= 1

    def run(self, name, e):
        waited = {}
        for s in self.order[name]:
            for sem, count in s.waits:
                if waited.get(sem, 0) < count:
                    waited[sem] = count
                    e.wait_ge(self.sems[sem], count)
            s.issue(e).then_inc(self.sems[s.completion[0]], s.by)
            if s.after is not None:
                s.after(e)
        for sem, count in (t for engine, t in self.at_end if engine == name):
            e.wait_ge(self.sems[sem], count)


def build(nc, x, ctx_in, gate_w, beta, gate_proj, up_proj, down_proj, shared_gate, shared_up,
          shared_down, out, sorted_rows):
    B, T, D = x.shape
    E, _, M = gate_proj.shape
    N = B * T
    MC = M // P
    K = 2
    GT = 4
    GN = GT * P
    NB = GN // T
    G = N // GN
    SCALE = float(D) ** -0.5
    ROW = D + 1 + K
    LIST = N + P
    CHOICE = E * LIST + P
    TILES = (N + E * (P - 1)) // P
    NO_TOKEN = 1 << 24
    WN = 2 * (2 * M + MC * D)
    assert T == 64 and D == P and M == 2 * P

    x_rows = x.rearrange("b s d -> (b s) d").rearrange("(g t p) d -> g p t d", g=G, t=GT)
    out_flat = out.rearrange("b s d -> (b s) d")
    out_rows = out_flat.rearrange("(g t p) d -> g p t d", g=G, t=GT)
    ctx_rows = ctx_in.rearrange("(g b) s d -> g s b d", g=G)

    with ExitStack() as ctx:
        prog = Program(nc, ctx)
        do, load = prog.do, prog.load

        def sb(name, shape, dt=F32):
            return ctx.enter_context(nc.sbuf_tensor(name, shape, dt))

        def bank(name):
            return ctx.enter_context(nc.psum_tensor(name, [P, 512], F32))

        ident = sb("ident", [P, P])
        ident_bf = sb("ident_bf", [P, P], BF16)
        ones_bf = sb("ones_bf", [P, P], BF16)
        before_bf = sb("before_bf", [P, P], BF16)
        last_row = sb("last_row", [P, P])
        mask = sb("mask", [P, GT, T], BF16)
        minus_half = sb("minus_half", [P, GT])
        expert_number = sb("expert_number", [P, E])
        list_start = sb("list_start", [P, K, E])
        tile_number = sb("tile_number", [P, 1])
        choice_start = sb("choice_start", [P, K])
        ones_e = sb("ones_e", [P, E])
        padding = sb("padding", [P, ROW])
        beta_all = sb("beta_all", [P, E])
        staged = sb("staged", [P, 3, 2 * M + MC * D])
        W = sb("W", [P, (E + 1) * WN], F32R)
        GU_HI, GU_LO, DN_HI, DN_LO = 0, 2 * M, 4 * M, 4 * M + MC * D
        router = sb("router", [E, D])
        router_T = sb("router_T", [D, E])
        router_hi = sb("router_hi", [D, E], F32R)
        router_lo = sb("router_lo", [D, E], F32R)
        x_sb = sb("x_sb", [P, 4, GT, D])
        c_sb = sb("c_sb", [T, 4, NB, D])
        stats = sb("stats", [P, 2, GT, 6])
        moments = sb("moments", [P, 2, GT, 2])
        var_eps = sb("var_eps", [P, 2, GT])
        rstd = sb("rstd", [P, 2, GT])
        shift = sb("shift", [P, 2, GT])
        xn = sb("xn", [P, GT, D])
        xn_T = sb("xn_T", [D, GN])
        ctx_T = sb("ctx_T", [D, NB, T])
        neg_max = sb("neg_max", [P, GT])
        exp_bias = sb("exp_bias", [P, GT])
        probs = sb("probs", [P, GT, T])
        row_sum = sb("row_sum", [P, GT])
        inv_sum = sb("inv_sum", [P, GT])
        probs_T = sb("probs_T", [T, GN])
        x2 = sb("x2", [P, 4, GT, D])
        rows = sb("rows", [P, 4, GT, ROW])
        xn2_hi = sb("xn2_hi", [D, 4, GN], F32R)
        xn2_lo = sb("xn2_lo", [D, 4, GN], F32R)
        biased = sb("biased", [P, GT, E])
        top8 = sb("top8", [P, GT, 8])
        top_index = sb("top_index", [P, GT, 8], U32)
        tanh_l = sb("tanh_l", [P, GT, E])
        tanh_c = sb("tanh_c", [P, GT, K])
        chosen = sb("chosen", [P, GT, K, E], BF16)
        list_next = sb("list_next", [P, K, E])
        picked = sb("picked", [P, GT, K, E])
        rank = sb("rank", [P, GT, K, E])
        slot_f = sb("slot_f", [P, GT, K])
        slot = sb("slot", [P, 4, GT, K], I32)
        th = sb("th", [P, MC, GN])
        gated = sb("gated", [P, MC, GN])
        hid = sb("hid", [P, MC, GN])
        hid_hi = sb("hid_hi", [P, MC, GN], F32R)
        hid_lo = sb("hid_lo", [P, MC, GN], F32R)
        acc = sb("acc", [P, 2, GT, D])
        count = sb("count", [P, K, E])
        count_i = sb("count_i", [P, K, E], I32)
        tiles_i = sb("tiles_i", [P, K, E], I32)
        tiles_f = sb("tiles_f", [P, K, E])
        until = sb("until", [P, K, E])
        past = sb("past", [P, K, E])
        past_tiles = sb("past_tiles", [P, K, E])
        expert = sb("expert", [P, K])
        tiles_before = sb("tiles_before", [P, K])
        table = sb("table", [P, 2, K])
        table_row = sb("table_row", [1, 2 * K, P], I32)
        list_end = sb("list_end", [1, K, E], I32)
        NR = 16
        AHEAD = 6
        tile_in = sb("tile_in", [P, NR, ROW])
        tx_hi = sb("tx_hi", [D, 2, 2, P], F32R)
        tx_lo = sb("tx_lo", [D, 2, 2, P], F32R)
        t_silu = sb("t_silu", [P, 2, M])
        t_hid = sb("t_hid", [P, 2, 2, M])
        th_hi = sb("th_hi", [P, 2, 2 * M], F32R)
        th_lo = sb("th_lo", [P, 2, 2 * M], F32R)
        t_out = sb("t_out", [P, NR, D])

        gu_pair = [ctx.enter_context(nc.psum_tensor(f"gu_pair{i}", [P, 2, 512], F32)) for i in range(2)]
        banks = [gu_pair[i // 2][:, i % 2] for i in range(4)] + [bank(f"bank{i}")[:, :] for i in range(4, 8)]

        steps = [
            lambda e: e.memset(ident[:], 0.0),
            lambda e: e.affine_select(out=ident[:], in_=ident[:], compare_op=ALU.not_equal, fill=1.0,
                                      base=0, pattern=[[-1, P]], channel_multiplier=1),
            lambda e: e.tensor_copy(ident_bf[:], ident[:]),
            lambda e: e.memset(ones_bf[:], 1.0),
            lambda e: e.affine_select(out=before_bf[:], in_=ones_bf[:], compare_op=ALU.is_gt, fill=0.0,
                                      base=0, pattern=[[1, P]], channel_multiplier=-1),
            lambda e: e.memset(mask[:], 0.0)]
        for half in range(2):
            part = mask[half * T:(half + 1) * T]
            steps.append(lambda e, part=part: e.affine_select(
                out=part, in_=part, compare_op=ALU.is_ge, fill=MASKED, base=0,
                pattern=[[0, GT], [-1, T]], channel_multiplier=1))
        imprecise = dict(allow_small_or_imprecise_dtypes=True)
        steps += [
            lambda e: e.memset(minus_half[:], -0.5),
            lambda e: e.iota(expert_number[:], pattern=[[1, E]], base=0, channel_multiplier=0, **imprecise),
            lambda e: e.iota(list_start[:], pattern=[[0, K], [LIST, E]], base=0, channel_multiplier=0, **imprecise),
            lambda e: e.iota(tile_number[:], pattern=[[0, 1]], base=0, channel_multiplier=1, **imprecise),
            lambda e: e.memset(ones_e[:], 1.0),
            lambda e: e.memset(choice_start[:, 0:1], 0.0),
            lambda e: e.memset(choice_start[:, 1:2], float(CHOICE)),
            lambda e: e.memset(padding[:], 0.0),
            lambda e: e.memset(padding[:, D:D + 1].bitcast(I32), NO_TOKEN),
            lambda e: e.memset(last_row[:], 0.0),
            lambda e: e.affine_select(out=last_row[:], in_=last_row[:], compare_op=ALU.not_equal, fill=1.0,
                                      base=1 - P, pattern=[[0, P]], channel_multiplier=1)]
        constants = None
        for step in steps:
            constants = do("pool", [constants], step, "const")
        shifted = do("dve", [constants], lambda e: e.tensor_scalar(
            list_start[:, 1], list_start[:, 1], float(CHOICE), None, ALU.add), "list_start")
        shifted = do("dve", [shifted], lambda e: e.tensor_copy(list_next[:, :, :], list_start[:, :, :]), "list_start")

        done = {}

        def at(name, g):
            return done[name, g] if g >= 0 else None

        def load_group(g):
            done["x_in", g] = load("sp", [at("x2", g - 4)], x_sb[:, g % 4], x_rows[g], f"x_in{g % 4}")
            done["c_in", g] = load("sp", [at("attended", g - 4)], c_sb[:, g % 4], ctx_rows[g], f"c_in{g % 4}")

        load_group(0)
        router_in = load("sp", [], router[:], gate_w, "router_in")
        beta_in = load("sp", [], beta_all[:], beta.rearrange("(a e) -> a e", a=1).broadcast_to([P, E]), "beta_in")
        load_group(1)
        for k in range(K):
            padded = load("act", [constants], sorted_rows[k * CHOICE + E * LIST:(k + 1) * CHOICE, :],
                          padding[:], "padding_out")
        sources = [(gate_proj[i], up_proj[i], down_proj[i]) for i in range(E)] + [
            (shared_gate[0], shared_up[0], shared_down[0])]

        def load_weights(j, ex):
            b = j % 3
            free = [done.get(("w_lo", j - 3))]
            load("sp", free, staged[:, b, 0:M], sources[ex][0], f"w_in{b}")
            load("sp", free, staged[:, b, M:2 * M], sources[ex][1], f"w_in{b}")
            done["w_in", j] = load("sp", free, staged[:, b, 2 * M:].rearrange("p (c h) -> p c h", c=MC),
                                   sources[ex][2].rearrange("(c p) h -> p c h", c=MC), f"w_in{b}")

        def split_weights(j, ex):
            b, w = j % 3, ex * WN
            pieces = [(0, 2 * M, w + GU_HI, w + GU_LO), (2 * M, 2 * M + MC * D, w + DN_HI, w + DN_LO)]

            def hi(e):
                for a, z, h, _ in pieces:
                    r = e.activation(W[:, h:h + z - a], staged[:, b, a:z], ACT.Copy)
                return r
            h = do("act", [done["w_in", j]], hi, "w_hi", ns=900)

            def lo(e):
                for a, z, h, l in pieces:
                    r = e.tensor_tensor(W[:, l:l + z - a], staged[:, b, a:z],
                                        W[:, h:h + z - a].bitcast(F32), ALU.subtract)
                return r
            done["w_lo", j] = do("dve" if ex == E else "pool", [h], lo, f"w_lo{int(ex == E)}")

        r = do("pe", [router_in, constants],
               lambda e: e.transpose(banks[3][:, 0:E], router[:], ident[0:E, 0:E]), "router_T")
        r = do("dve", [r], lambda e: e.tensor_copy(router_T[:], banks[3][:, 0:E]), "router_T_copy")
        r = do("dve", [r], lambda e: e.tensor_copy(router_hi[:], router_T[:]), "router_hi")
        router_done = do("dve", [r], lambda e: e.tensor_tensor(
            router_lo[:], router_T[:], router_hi[:].bitcast(F32), ALU.subtract), "router_lo")

        def mean_and_rstd(g, n, src, waits, free):
            def st(e):
                for i in range(GT):
                    r = e.bn_stats(stats[:, n, i], src[:, i])
                return r
            a = do("dve", waits + [at(f"moments{n}", g - 1)], st, f"stats{n}", ns=820)

            def ag(e):
                for i in range(GT):
                    r = e.bn_aggr(moments[:, n, i], stats[:, n, i])
                return r
            b = done[f"moments{n}", g] = do("dve", [a, free], ag, f"moments{n}", ns=310)
            c = do("dve", [b, at(f"rstd{n}", g - 1)], lambda e: e.tensor_scalar(
                var_eps[:, n], moments[:, n, :, 1], EPS, None, ALU.add), f"var_eps{n}", ns=72)
            c = do("pool", [c, free], lambda e: e.tensor_tensor(
                rstd[:, n], var_eps[:, n], minus_half[:], ALU.pow), f"rstd{n}", ns=960)
            done[f"rstd{n}", g] = do("dve", [b, c, free], lambda e: e.scalar_tensor_tensor(
                out=shift[:, n], in0=moments[:, n, :, 0], scalar=-1.0, in1=rstd[:, n], op0=ALU.mult, op1=ALU.mult),
                f"shift{n}", ns=72)

        def normalise(g, n, dst, src, waits):
            def nm(e):
                for i in range(GT):
                    r = e.activation(dst[:, i], src[:, i], ACT.Identity, bias=shift[:, n, i:i + 1],
                                     scale=rstd[:, n, i:i + 1])
                return r
            done[f"normal{n}", g] = do("act", [done[f"rstd{n}", g]] + waits, nm, f"normal{n}", ns=1170)

        def group_steps(g):
            A, C, O, X = banks[0:4]
            b4, b2 = g % 4, g % 2
            mean_and_rstd(g, 0, x_sb[:, b4], [done["x_in", g]], at("normal0", g - 1))

            normalise(g, 0, xn, x_sb[:, b4], [at("xn_transposed", g - 1)])

            def tc(e):
                for b in range(NB):
                    r = e.transpose(C[:, b * T:(b + 1) * T], c_sb[:, b4, b], ident[0:T, 0:T])
                return r
            t = do("pe", [done["c_in", g], constants, at("probs_T", g - 1)], tc, "ctx_transposed", ns=430)
            done["ctx_T", g] = do("act", [t, at("scores", g - 1)], lambda e: e.activation(
                ctx_T[:, :, :], C[:, :].rearrange("p (b s) -> p b s", b=NB), ACT.Copy), "ctx_T", ns=520)

            def tx(e):
                for i in range(GT):
                    r = e.transpose(A[:, i * P:(i + 1) * P], xn[:, i], ident[:])
                return r
            t = done["xn_transposed", g] = do("pe", [done["normal0", g], at("exp", g - 1)], tx, "xn_transposed", ns=430)
            done["xn_T", g] = do("act", [t, at("scores", g - 1)],
                                 lambda e: e.activation(xn_T[:], A[:], ACT.Copy), "xn_T", ns=520)

            def sc(e):
                e.matmul(A[:, 0:GT * T], ident_bf[:], mask[:, :, :].rearrange("p t k -> p (t k)"),
                         start=True, stop=False, skip_group_check=True)
                for i in range(GT):
                    for half in range(2):
                        q = xn_T[:, i * P + half * T:i * P + (half + 1) * T]
                        r = e.matmul(A[half * T:(half + 1) * T, i * T:(i + 1) * T], q, ctx_T[:, 2 * i + half],
                                     start=False, stop=True, skip_group_check=True)
                return r
            done["scores", g] = do("pe", [done["xn_T", g], done["ctx_T", g]], sc, "scores", ns=1100)
            S = A[:, 0:GT * T].rearrange("p (t k) -> p t k", t=GT)
            mx = do("dve", [done["scores", g], at("exp_bias", g - 1)],
                    lambda e: e.tensor_reduce(neg_max[:], S, AX_X, ALU.max, negate=True), "row_max", ns=340)
            done["exp_bias", g] = do("dve", [mx, at("exp", g - 1)], lambda e: e.tensor_scalar(
                exp_bias[:], neg_max[:], SCALE, None, ALU.mult), "exp_bias", ns=72)

            def ex(e):
                for i in range(GT):
                    r = e.activation(probs[:, i], S[:, i], ACT.Exp, bias=exp_bias[:, i:i + 1], scale=SCALE,
                                     accum_out=row_sum[:, i:i + 1])
                return r
            done["exp", g] = do("act", [done["exp_bias", g], at("probs_transposed", g - 1), at("inv_sum", g - 1)],
                                ex, "exp", ns=1250)
            done["inv_sum", g] = do("dve", [done["exp", g], at("x2", g - 1)],
                                    lambda e: e.reciprocal(inv_sum[:], row_sum[:]), "inv_sum", ns=95)

            def tp(e):
                for i in range(GT):
                    r = e.transpose(C[0:T, i * P:(i + 1) * P], probs[:, i], ident[:])
                return r
            t = done["probs_transposed", g] = do("pe", [done["exp", g], done["ctx_T", g]], tp, "probs_transposed", ns=430)
            done["probs_T", g] = do("act", [t, at("attended", g - 1)],
                                    lambda e: e.activation(probs_T[:], C[0:T, :], ACT.Copy), "probs_T", ns=520)

            def pv(e):
                for i in range(GT):
                    for half in range(2):
                        r = e.matmul(O[half * T:(half + 1) * T, i * D:(i + 1) * D],
                                     probs_T[:, i * P + half * T:i * P + (half + 1) * T],
                                     c_sb[:, b4, 2 * i + half], start=True, stop=True, skip_group_check=True)
                return r
            done["attended", g] = do("pe", [done["probs_T", g], at("x2", g - 1), at("summed", g - BEHIND)], pv, "attended", ns=1750)

            def rs(e):
                for i in range(GT):
                    r = e.scalar_tensor_tensor(out=x2[:, b4, i], in0=O[:, i * D:(i + 1) * D],
                                               scalar=inv_sum[:, i:i + 1], in1=x_sb[:, b4, i],
                                               op0=ALU.mult, op1=ALU.add)
                return r
            done["x2", g] = do("dve", [done["attended", g], done["inv_sum", g], at("summed", g - 4)], rs, "x2", ns=1040)
            mean_and_rstd(g, 1, x2[:, b4], [done["x2", g]], at("normal1", g - 1))

            sent = at("scattered", g - 4)
            normalise(g, 1, rows[:, b4, :, 0:D], x2[:, b4], [sent, constants])
            done["token_number", g] = do("pool", [sent, constants], lambda e: e.iota(
                rows[:, b4, :, D:D + 1].bitcast(I32), pattern=[[P, GT], [0, 1]], base=g * GN,
                channel_multiplier=1), "token_number", ns=94)

            def tx2(e):
                for i in range(GT):
                    r = e.transpose(X[:, i * P:(i + 1) * P], rows[:, b4, i, 0:D], ident[:])
                return r
            t = do("pe", [done["normal1", g], router_done, at("rank", g - 1), at("list_next", g - 1)], tx2, "xn2_transposed", ns=430)
            hi = do("act", [t, at("gate_up1", g - 4), at("xn2_lo", g - 4)],
                    lambda e: e.activation(xn2_hi[:, b4], X[:], ACT.Copy), "xn2_hi", ns=520)
            done["xn2_lo", g] = do("dve", [hi, at("gate_up1", g - 4)], lambda e: e.tensor_tensor(
                xn2_lo[:, b4], X[:], xn2_hi[:, b4].bitcast(F32), ALU.subtract), "xn2_lo", ns=610)

            def lg(e):
                for i in range(GT):
                    s = slice(i * P, (i + 1) * P)
                    parts = ((xn2_hi, router_hi), (xn2_hi, router_lo), (xn2_lo, router_hi))
                    for j, (a, b) in enumerate(parts):
                        r = e.matmul(X[:, i * E:(i + 1) * E], a[:, b4, s], b[:], start=(j == 0), stop=(j == 2))
                return r
            t = do("pe", [done["xn2_lo", g]], lg, "logits_mm", ns=650)
            L = X[:, 0:GT * E].rearrange("p (t e) -> p t e", t=GT)
            a = do("dve", [t, beta_in, at("top_index", g - 1)], lambda e: e.tensor_tensor(
                biased[:, :, :], L,
                beta_all[:, :].rearrange("p (a e) -> p a e", a=1).broadcast_to([P, GT, E]), ALU.add), "biased", ns=102)
            th_l = done["tanh_logits", g] = do("act", [t, a, at("picked", g - 1)], lambda e: e.activation(
                tanh_l[:, :, :], L, ACT.Tanh, scale=0.5), "tanh_logits", ns=200)

            def mx8(e):
                for i in range(GT):
                    r = e.max(top8[:, i], biased[:, i])
                return r
            b = do("dve", [a], mx8, "top8", ns=310)

            def mi(e):
                for i in range(GT):
                    r = e.max_index(top_index[:, i], top8[:, i], biased[:, i])
                return r
            b = done["top_index", g] = do("dve", [b, at("one_hot", g - 1)], mi, "top_index", ns=310)
            hot = done["one_hot", g] = do("dve", [b, constants, at("rank_mm", g - 1), at("list_next", g - 1),
                                                  at("slot", g - 1)], lambda e: e.tensor_tensor(
                chosen[:, :, :, :],
                expert_number[:, :].rearrange("p (a c e) -> p a c e", a=1, c=1).broadcast_to([P, GT, K, E]),
                top_index[:, :, 0:K].rearrange("p t (k a) -> p t k a", a=1).broadcast_to([P, GT, K, E]),
                ALU.is_equal), "one_hot", ns=140)

            def rk(e):
                KE = K * E
                R = X[:, 64:64 + GT * KE]
                flat = chosen[:, :, :, :].rearrange("p t k e -> p t (k e)")
                e.matmul(R, before_bf[:], flat.rearrange("p t n -> p (t n)"), start=True, stop=False,
                         skip_group_check=True)
                for i in range(GT):
                    for j in range(i):
                        e.matmul(R[:, i * KE:(i + 1) * KE], ones_bf[:], flat[:, j], start=False, stop=False,
                                 skip_group_check=True)
                    r = e.matmul(R[:, i * KE:(i + 1) * KE], last_row[:],
                                 list_next[:, :, :].rearrange("p k e -> p (k e)"), start=False, stop=True,
                                 skip_group_check=True)
                return r
            done["rank_mm", g] = do("pe", [hot, at("list_next", g - 1), a, th_l, shifted], rk, "rank_mm", ns=750)
            p = done["picked", g] = do("dve", [hot, th_l, at("weights", g - 1)], lambda e: e.tensor_tensor(
                picked[:, :, :, :], chosen[:, :, :, :],
                tanh_l[:, :, :].rearrange("p t (a e) -> p t a e", a=1).broadcast_to([P, GT, K, E]), ALU.mult),
                "picked", ns=135)
            p = do("dve", [p, at("weights", g - 1)], lambda e: e.tensor_reduce(
                tanh_c[:, :, :], picked[:, :, :, :], AX_X, ALU.add), "tanh_chosen", ns=135)
            done["weights", g] = do("dve", [p, sent], lambda e: e.tensor_scalar(
                rows[:, b4, :, D + 1:D + 1 + K], tanh_c[:, :, :], 0.5, 0.5, ALU.mult, ALU.add), "weights", ns=72)

            R = X[:, 64:64 + GT * K * E].rearrange("p (t k e) -> p t k e", t=GT, k=K)
            t = done["rank", g] = do("dve", [done["rank_mm", g], at("slot", g - 1)], lambda e: e.tensor_tensor(
                rank[:, :, :, :], chosen[:, :, :, :], R, ALU.mult), "rank", ns=190)
            done["list_next", g] = do("dve", [done["rank_mm", g]], lambda e: e.tensor_tensor(
                list_next[:, :, :], chosen[:, GT - 1], R[:, GT - 1], ALU.add), "list_next", ns=140)
            t = do("dve", [t, at("slot", g - 1)], lambda e: e.tensor_reduce(
                slot_f[:, :, :], rank[:, :, :, :], AX_X, ALU.add), "slot_f", ns=135)
            done["slot", g] = do("dve", [t, sent], lambda e: e.tensor_copy(slot[:, b4], slot_f[:, :, :]), "slot", ns=75)

            waits = [done["slot", g], done["weights", g], done["normal1", g], done["token_number", g]]
            for i in range(GT):
                for k in range(K):
                    done["scattered", g] = do("pool", waits, lambda e, i=i, k=k: e.indirect_dma_start(
                        sorted_rows, bass.IndirectOffsetOnAxis(ap=slot[:, b4, i, k:k + 1], axis=0),
                        rows[:, b4, i, :], None), f"scattered{b4}", 16, 1040, late=400)

        def shared_steps(g):
            O = banks[2]
            b4, b2 = g % 4, g % 2
            for m in range(MC):
                gate, up = banks[4 + 2 * m], banks[5 + 2 * m]

                def mm(e, m=m, gate=gate, up=up):
                    for k, dst in enumerate((gate, up)):
                        c = E * WN + k * M + m * P
                        w = [W[:, c + GU_HI:c + GU_HI + P], W[:, c + GU_LO:c + GU_LO + P]]
                        parts = ((w[0], xn2_hi), (w[0], xn2_lo), (w[1], xn2_hi))
                        for j, (lhs, rhs) in enumerate(parts):
                            r = e.matmul(dst[:], lhs, rhs[:, b4], start=(j == 0), stop=(j == 2))
                    return r
                free = at(f"hid{m}", g - 1)
                t = done[f"gate_up{m}", g] = do("pe", [done["xn2_lo", g], done["w_lo", 0], free], mm, f"gate_up{m}", ns=1300)
                t2 = done[f"tanh{m}", g] = do("act", [t, at(f"gated{m}", g - 1)], lambda e, m=m, gate=gate: e.activation(
                    th[:, m], gate[:], ACT.Tanh, scale=0.5), f"tanh{m}", ns=480)
                t2 = done[f"gated{m}", g] = do("dve", [t2, at(f"hid{m}", g - 1)], lambda e, m=m, gate=gate:
                    e.scalar_tensor_tensor(out=gated[:, m], in0=th[:, m], scalar=1.0, in1=gate[:],
                                           op0=ALU.add, op1=ALU.mult), f"gated{m}", ns=610)
                t2 = done[f"hid{m}", g] = do("dve", [t2, at(f"hid_lo{m}", g - 1)], lambda e, m=m, up=up:
                    e.tensor_tensor(hid[:, m], gated[:, m], up[:], ALU.mult), f"hid{m}", ns=610)
                t2 = do("act", [t2, at("down", g - 1)],
                        lambda e, m=m: e.activation(hid_hi[:, m], hid[:, m], ACT.Copy), f"hid_hi{m}", ns=560)
                done[f"hid_lo{m}", g] = do("dve", [t2, at("down", g - 1)], lambda e, m=m: e.tensor_tensor(
                    hid_lo[:, m], hid[:, m], hid_hi[:, m].bitcast(F32), ALU.subtract), f"hid_lo{m}", ns=610)

            def dn(e):
                for t in range(GT):
                    j = 0
                    for m in range(MC):
                        h = [v[:, m, t * P:(t + 1) * P] for v in (hid_hi, hid_lo)]
                        c = E * WN + m * D
                        w = [W[:, c + DN_HI:c + DN_HI + D], W[:, c + DN_LO:c + DN_LO + D]]
                        for lhs, rhs in ((h[0], w[0]), (h[0], w[1]), (h[1], w[0])):
                            r = e.matmul(O[:, t * D:(t + 1) * D], lhs, rhs, start=(j == 0), stop=(j == 5))
                            j += 1
                return r
            done["down", g] = do("pe", [done["hid_lo0", g], done["hid_lo1", g], done["x2", min(g + BEHIND - 1, G - 1)]], dn, "down", ns=2600)
            done["summed", g] = do("dve", [done["down", g], at("stored", g - 2)], lambda e:
                e.scalar_tensor_tensor(out=acc[:, b2].rearrange("p t d -> p (t d)"), in0=O, scalar=0.5,
                                       in1=x2[:, b4].rearrange("p t d -> p (t d)"), op0=ALU.mult, op1=ALU.add),
                "summed", ns=610)
            done["stored", g] = load("sp", [done["summed", g]], out_rows[g], acc[:, b2], f"stored{b2}")

        load_weights(0, E)
        split_weights(0, E)
        order = [E] + list(range(E))
        BEHIND = 3
        for g in range(G):
            if 2 <= g + 1 < G:
                load_group(g + 1)
            if 1 <= g <= E:
                load_weights(g, order[g])
                split_weights(g, order[g])
            if g >= BEHIND:
                shared_steps(g - BEHIND)
            group_steps(g)
        for g in range(G - BEHIND, G):
            shared_steps(g)

        last = G - 1
        X = banks[3]
        t = do("pe", [done["list_next", last], done["rank", last], done["slot", last]], lambda e: e.matmul(
            X[:, 0:K * E], last_row[:], list_next[:, :, :].rearrange("p k e -> p (k e)"), start=True, stop=True), "ends")
        ends_mm = X[:, 0:K * E].rearrange("p (k e) -> p k e", k=K)
        ends = do("dve", [t], lambda e: e.tensor_copy(list_end[:, :, :], ends_mm[0:1]), "table")
        t0 = do("dve", [t], lambda e: e.tensor_tensor(count[:, :, :], ends_mm, list_start[:, :, :], ALU.subtract), "table")
        t = do("dve", [t0], lambda e: e.tensor_scalar(count_i[:, :, :], count[:, :, :], float(P - 1), None, ALU.add), "table")
        t = do("dve", [t], lambda e: e.tensor_scalar(tiles_i[:, :, :], count_i[:, :, :], 7, None,
                                                     ALU.arith_shift_right), "table")
        t = do("dve", [t], lambda e: e.tensor_copy(tiles_f[:, :, :], tiles_i[:, :, :]), "table")
        for k in range(K):
            t = do("dve", [t], lambda e, k=k: e.tensor_tensor_scan(
                until[:, k], ones_e[:], tiles_f[:, k], 0.0, ALU.mult, ALU.add), "table")
        t = do("dve", [t], lambda e: e.tensor_scalar(past[:, :, :], until[:, :, :], tile_number[:, 0:1], None,
                                                     ALU.is_le), "table")
        u = do("dve", [t], lambda e: e.tensor_reduce(expert[:], past[:, :, :], AX_X, ALU.add), "table")
        t = do("dve", [t], lambda e: e.tensor_tensor(past_tiles[:, :, :], past[:, :, :], tiles_f[:, :, :], ALU.mult), "table")
        t = do("dve", [t], lambda e: e.tensor_reduce(tiles_before[:], past_tiles[:, :, :], AX_X, ALU.add), "table")
        t = do("dve", [t], lambda e: e.tensor_scalar(tiles_before[:], tiles_before[:], tile_number[:, 0:1], -float(P),
                                                     ALU.subtract, ALU.mult), "table")
        t = do("dve", [t, u], lambda e: e.scalar_tensor_tensor(
            out=table[:, 0], in0=expert[:], scalar=float(LIST), in1=tiles_before[:], op0=ALU.mult, op1=ALU.add), "table")
        t = do("dve", [t], lambda e: e.scalar_tensor_tensor(
            out=table[:, 0], in0=table[:, 0], scalar=float(E * LIST), in1=choice_start[:], op0=ALU.min, op1=ALU.add), "table")
        t = do("dve", [t], lambda e: e.tensor_scalar(table[:, 1], expert[:], float(E - 1), float(WN),
                                                     ALU.min, ALU.mult), "table")

        def tr(e):
            for i in range(2 * K):
                r = e.matmul(X[0:1, i * P:(i + 1) * P], table[:, i // K, i % K:i % K + 1], ident[:],
                             start=True, stop=True)
            return r
        t = do("pe", [t, t0, ends], tr, "table_T")
        table_done = do("dve", [t], lambda e: e.tensor_copy(
            table_row[:, :, :].rearrange("p n j -> p (n j)"), X[0:1, 0:2 * K * P]), "table")

        for k in range(K):
            for ex in range(E):
                def pad(e, k=k, ex=ex):
                    v = e.value_load(list_end[0:1, k, ex:ex + 1], min_val=0, max_val=K * CHOICE - P)
                    return e.dma_start(sorted_rows[bass.ds(v, P), :], padding[:])
                padded = do(("sp", "act")[ex % 2], [ends, constants], pad, f"padded{ex % 2}", 16)
                done["padded", ex % 2] = padded

        sorted_done = [done["scattered", g] for g in range(G - 4, G)] + [
            done["padded", 0], done["padded", 1], (("padding_out"), 32)]
        out_written = [done["stored", G - 1], done["stored", G - 2]]
        pairs = K * TILES // 2
        assert K * TILES % 2 == 0
        tok = {}

        def t_at(name, i):
            return tok[name, i] if i >= 0 else None

        def t_load(j):
            k, n = divmod(j, TILES)

            def ld(e):
                v = e.value_load(table_row[0:1, k, n:n + 1], min_val=0, max_val=K * CHOICE - P)
                return e.dma_start(tile_in[:, j % NR], sorted_rows[bass.ds(v, P), :])
            tok["t_in", j] = do("sp", [table_done] + sorted_done + [t_at("t_added", j - NR)], ld, f"t_in{j % NR}", 16, 1060)

        def t_transpose(i):
            def tr(e):
                for h in range(2):
                    r = e.transpose(banks[4][:, h * P:(h + 1) * P], tile_in[:, (2 * i + h) % NR, 0:D], ident[:])
                return r
            first = [done["summed", last]] if i == 0 else []
            t = do("pe", [tok["t_in", 2 * i], tok["t_in", 2 * i + 1], t_at("tx_lo", i - 1)] + first, tr, "t_transposed", ns=215)
            src = banks[4][:, 0:2 * P].rearrange("p (h n) -> p h n", h=2)
            hi = do("act", [t, t_at("t_gate_up", i - 2), t_at("tx_lo", i - 2)],
                    lambda e: e.activation(tx_hi[:, i % 2], src, ACT.Copy), "tx_hi", ns=265)
            tok["tx_lo", i] = do("dve", [hi, t_at("t_gate_up", i - 2)], lambda e: e.tensor_tensor(
                tx_lo[:, i % 2], src, tx_hi[:, i % 2].bitcast(F32), ALU.subtract), "tx_lo", ns=340)

        offsets = {}

        def t_offsets(i):
            def ld(e):
                for h in range(2):
                    k, n = divmod(2 * i + h, TILES)
                    offsets[2 * i + h] = e.value_load(table_row[0:1, K + k, n:n + 1], min_val=0,
                                                      max_val=(E - 1) * WN)
            return ld

        def t_gate_up(i):
            gu = banks[0:2] if i % 2 else banks[2:4]
            earlier = {0: [done["w_lo", E], done["summed", last]], 1: [done["exp", last], done["probs_T", last]]}

            def mm(e):
                if i == 0:
                    t_offsets(0)(e)
                for h in range(2):
                    v = offsets[2 * i + h]
                    w = [W[:, bass.ds(v + GU_HI, 2 * M)], W[:, bass.ds(v + GU_LO, 2 * M)]]
                    for j, (lhs, rhs) in enumerate(((tx_hi, w[0]), (tx_lo, w[0]), (tx_hi, w[1]))):
                        r = e.matmul(gu[h][:], lhs[:, i % 2, h], rhs, start=(j == 0), stop=(j == 2))
                return r
            t = tok["t_gate_up", i] = do("pe", [tok["tx_lo", i], table_done, t_at("t_hid", i - 2)] +
                                         earlier.get(i, []), mm, "t_gate_up", ns=1300,
                                         after=t_offsets(i + 1) if i + 1 < pairs else None)
            g, u = pair_view[i % 2]
            t = do("act", [t, t_at("t_hid", i - 1), done["tanh1", last]], lambda e: e.activation(t_silu[:, :, :], g, ACT.Silu), "t_silu", ns=480)
            tok["t_hid", i] = do("dve", [t, t_at("th_transposed", i - 2)], lambda e: e.tensor_tensor(
                t_hid[:, i % 2], t_silu[:, :, :], u, ALU.mult), "t_hid", ns=610)

        def t_turn(i):
            H = banks[5 + i % 2]

            def tr(e):
                for h in range(2):
                    for m in range(MC):
                        c = (h * MC + m) * P
                        r = e.transpose(H[:, c:c + P], t_hid[:, i % 2, h, m * P:(m + 1) * P], ident[:])
                return r
            t = tok["th_transposed", i] = do("pe", [tok["t_hid", i], t_at("th_lo", i - 2), done["hid0", last], done["hid1", last]], tr, "th_transposed", ns=430)
            hi = do("act", [t, t_at("t_down", i - 2), t_at("th_lo", i - 2)],
                    lambda e: e.activation(th_hi[:, i % 2], H[:], ACT.Copy), "th_hi", ns=480)
            tok["th_lo", i] = do("dve", [hi, t_at("t_down", i - 2)], lambda e: e.tensor_tensor(
                th_lo[:, i % 2], H[:], th_hi[:, i % 2].bitcast(F32), ALU.subtract), "th_lo", ns=610)

        def t_down(i):
            def mm(e):
                for h in range(2):
                    v = offsets.pop(2 * i + h)
                    j = 0
                    for m in range(MC):
                        c = (h * MC + m) * P
                        hi, lo = th_hi[:, i % 2, c:c + P], th_lo[:, i % 2, c:c + P]
                        w = [W[:, bass.ds(v + (DN_HI + m * D), D)], W[:, bass.ds(v + (DN_LO + m * D), D)]]
                        for lhs, rhs in ((hi, w[0]), (lo, w[0]), (hi, w[1])):
                            r = e.matmul(banks[7][:, h * D:(h + 1) * D], lhs, rhs, start=(j == 0), stop=(j == 5))
                            j += 1
                return r
            t = tok["t_down", i] = do("pe", [tok["th_lo", i], t_at("t_out", i - 1), done["hid1", last]], mm, "t_down", ns=1300)
            for h in range(2):
                n = 2 * i + h
                k = n // TILES
                a = do("act", [t, t_at("t_added", n - NR)], lambda e, n=n, h=h, k=k: e.activation(
                    t_out[:, n % NR], banks[7][:, h * D:(h + 1) * D], ACT.Copy,
                    scale=tile_in[:, n % NR, D + 1 + k:D + 2 + k]), "t_out", ns=255)
                tok["t_out", i] = a
                order = [tok["t_added", q] for q in range(TILES - NR, TILES)] if k else []
                tok["t_added", n] = do("pool", [a] + out_written + order, lambda e, n=n: e.indirect_dma_start(
                    out_flat, bass.IndirectOffsetOnAxis(ap=tile_in[:, n % NR, D:D + 1].bitcast(I32), axis=0),
                    t_out[:, n % NR], None, bounds_check=N - 1, oob_is_err=False, compute_op=ALU.add),
                    f"t_added{n % NR}", 16, 1040)

        pair_view = []
        for b in (gu_pair[1], gu_pair[0]):
            v = b[:, :, :]
            pair_view.append((v[:, :, 0:M], v[:, :, M:2 * M]))
        for j in range(AHEAD):
            t_load(j)
        t_transpose(0)
        for i in range(pairs + 2):
            if i < pairs:
                for j in (2 * i + AHEAD, 2 * i + AHEAD + 1):
                    if j < 2 * pairs:
                        t_load(j)
                t_gate_up(i)
            if 1 <= i <= pairs:
                t_turn(i - 1)
            if i + 1 < pairs:
                t_transpose(i + 1)
            if i >= 2:
                t_down(i - 2)

        for t in [tok["t_added", q] for q in range(2 * pairs - NR, 2 * pairs)]:
            prog.at_end.append(("pool", t))
        prog.arrange()

        block = ctx.enter_context(nc.Block())

        @block.sync
        def _(e):
            prog.run("sp", e)

        @block.gpsimd
        def _(e):
            prog.run("pool", e)

        @block.scalar
        def _(e):
            prog.run("act", e)

        @block.vector
        def _(e):
            prog.run("dve", e)

        @block.tensor
        def _(e):
            prog.run("pe", e)


_INS = ["x", "ctx_1024", "L0_ffn_gate_w", "L0_ffn_beta", "L0_ffn_gate_proj_w", "L0_ffn_up_proj_w", "L0_ffn_down_proj_w",
        "L0_ffn_shared_gate_w", "L0_ffn_shared_up_w", "L0_ffn_shared_down_w"]


def kernel(**inputs):
    import numpy as np
    import concourse.bacc as bacc
    from concourse.bass_utils import run_bass_kernel_spmd

    nc = bacc.Bacc("TRN2", target_bir_lowering=False, num_devices=1)
    arrays, args = {}, []
    for name in _INS:
        a = np.ascontiguousarray(inputs[name])
        arrays[name] = a
        args.append(nc.dram_tensor(name, a.shape, mybir.dt.from_np(a.dtype), kind="ExternalInput").ap())
    shape = inputs["x"].shape
    args.append(nc.dram_tensor("out", shape, F32, kind="ExternalOutput").ap())
    T, (E, D) = shape[0] * shape[1], inputs["L0_ffn_gate_w"].shape
    args.append(nc.dram_tensor("sorted_rows", (2 * (E * (T + P) + P), D + 3), F32).ap())
    build(nc, *args)
    return run_bass_kernel_spmd(nc, [arrays], core_ids=[0]).results[0]["out"]
```

```python
from contextlib import ExitStack

import concourse.bass as bass
from concourse import mybir

F32 = mybir.dt.float32
F32R = mybir.dt.float32r
BF16 = mybir.dt.bfloat16
U32 = mybir.dt.uint32
I32 = mybir.dt.int32
ALU = mybir.AluOpType
ACT = mybir.ActivationFunctionType
AX_X = mybir.AxisListType.X

P = 128
EPS = 1e-5
MASKED = -1e30


class Step:
    def __init__(self, engine, waits, issue, completion, by, ns, after, behind, number):
        self.engine, self.issue, self.completion, self.by = engine, issue, completion, by
        self.waits = [t for t in waits if t is not None]
        self.behind = [t for t in behind if t is not None]
        self.ns, self.after, self.number = ns, after, number


class Program:
    LATENCY = 200
    DMA_LATENCY = 2200
    WINDOW = 150
    LOOKAHEAD = 160

    def __init__(self, nc, ctx):
        self.nc, self.ctx = nc, ctx
        self.steps = []
        self.order = {"pe": [], "act": [], "dve": [], "pool": [], "sp": []}
        self.sems, self.counts = {}, {}
        self.at_end = []

    def do(self, engine, waits, issue, signal, by=1, ns=100, after=None, behind=()):
        if signal not in self.sems:
            self.sems[signal] = self.ctx.enter_context(self.nc.semaphore("s_" + signal))
            self.counts[signal] = 0
        self.counts[signal] += by
        token = signal, self.counts[signal]
        self.steps.append(Step(engine, waits, issue, token, by, ns, after, behind, len(self.steps)))
        return token

    def load(self, engine, waits, out, in_, signal):
        return self.do(engine, waits, lambda e: e.dma_start(out, in_), signal, 16, 60)

    def arrange(self):
        free = {name: 0 for name in self.order}
        known = {}
        waiting = {name: [s for s in self.steps if s.engine == name] for name in self.order}
        chain = {s.completion: 0 for s in self.steps}
        for s in reversed(self.steps):
            for t in s.waits:
                chain[t] = max(chain[t], chain[s.completion] + s.ns + self.LATENCY)
        for _ in self.steps:
            ready = []
            for name, steps in waiting.items():
                seen = set()
                for s in steps[:self.LOOKAHEAD]:
                    if s.completion[0] in seen:
                        continue
                    seen.add(s.completion[0])
                    if all(t in known for t in s.waits + s.behind):
                        start = max([free[name]] + [known[t] for t in s.waits + s.behind])
                        ready.append((start, s.number, s))
            first, _, s = min(ready, key=lambda c: c[:2])
            rivals = [c for c in ready if c[2].engine == s.engine and c[0] <= first + self.WINDOW]
            start, _, s = max(rivals, key=lambda c: (chain[c[2].completion], -c[1]))
            free[s.engine] = start + s.ns
            known[s.completion] = start + s.ns + (self.DMA_LATENCY if s.by == 16 else self.LATENCY)
            waiting[s.engine].remove(s)
            self.order[s.engine].append(s)

    def run(self, name, e):
        waited = {}
        for s in self.order[name]:
            for sem, count in s.waits:
                if waited.get(sem, 0) < count:
                    waited[sem] = count
                    e.wait_ge(self.sems[sem], count)
            s.issue(e).then_inc(self.sems[s.completion[0]], s.by)
            if s.after is not None:
                s.after(e)
        for sem, count in (t for engine, t in self.at_end if engine == name):
            e.wait_ge(self.sems[sem], count)


def build(nc, x, ctx_in, gate_w, beta, gate_proj, up_proj, down_proj, shared_gate, shared_up,
          shared_down, out, sorted_rows):
    B, T, D = x.shape
    E, _, M = gate_proj.shape
    N = B * T
    MC = M // P
    K = 2
    GT = 4
    GN = GT * P
    NB = GN // T
    G = N // GN
    SCALE = float(D) ** -0.5
    ROW = D + 1 + K
    LIST = N + P
    CHOICE = E * LIST + P
    TILES = (N + E * (P - 1)) // P
    NO_TOKEN = 1 << 24
    WN = 2 * (2 * M + MC * D)
    assert T == 64 and D == P and M == 2 * P

    x_rows = x.rearrange("b s d -> (b s) d").rearrange("(g t p) d -> g p t d", g=G, t=GT)
    out_flat = out.rearrange("b s d -> (b s) d")
    out_rows = out_flat.rearrange("(g t p) d -> g p t d", g=G, t=GT)
    ctx_rows = ctx_in.rearrange("b s d -> (b s) d").rearrange("(g t p) d -> g p t d", g=G, t=GT)

    with ExitStack() as ctx:
        prog = Program(nc, ctx)
        do, load = prog.do, prog.load

        def sb(name, shape, dt=F32):
            return ctx.enter_context(nc.sbuf_tensor(name, shape, dt))

        def bank(name):
            return ctx.enter_context(nc.psum_tensor(name, [P, 512], F32))

        LEAD = 3
        ident = sb("ident", [P, P])
        ident_bf = sb("ident_bf", [P, P], BF16)
        ones_bf = sb("ones_bf", [P, P], BF16)
        before_bf = sb("before_bf", [P, P], BF16)
        last_row = sb("last_row", [P, P])
        mask = sb("mask", [P, GT, T], BF16)
        minus_half = sb("minus_half", [P, 2, GT])
        expert_number = sb("expert_number", [P, E])
        list_start = sb("list_start", [P, K, E])
        tile_number = sb("tile_number", [P, 1])
        choice_start = sb("choice_start", [P, K])
        ones_e = sb("ones_e", [P, E])
        padding = sb("padding", [P, ROW])
        beta_all = sb("beta_all", [P, E])
        WARM = 32
        warm = sb("warm", [P, GN], BF16)
        RANKS = P
        staged = sb("staged", [P, 3, 2 * M + MC * D])
        W = sb("W", [P, (E + 1) * WN], F32R)
        GU_HI, GU_LO = 0, 2 * M
        DN_HI, DN_LO = 4 * M, 4 * M + D
        shared_dn = sb("shared_dn", [P, MC, D])
        router = sb("router", [E, D])
        router_T = sb("router_T", [D, E])
        router_parts = sb("router_parts", [D, 2 * E], F32R)
        RX, RC = 5, 4
        x_sb = sb("x_sb", [P, RX, GT, D])
        c_sb = sb("c_sb", [P, RC, GT, D])
        DEFER = RR = 6
        NS = 4
        stats = sb("stats", [P, 2, GT, 6])
        moments = sb("moments", [P, NS, 2, GT, 2])
        var_eps = sb("var_eps", [P, NS, 2, GT])
        rstd = sb("rstd", [P, NS, 2, GT])
        shift = sb("shift", [P, NS, 2, GT])
        xn = sb("xn", [P, GT, D])
        xn_T = sb("xn_T", [D, GN])
        ctx_T = sb("ctx_T", [D, NB, T])
        neg_max = sb("neg_max", [P, GT])
        exp_bias = sb("exp_bias", [P, GT])
        probs = sb("probs", [P, GT, T])
        row_sum = sb("row_sum", [P, GT])
        inv_sum = sb("inv_sum", [P, GT])
        probs_T = sb("probs_T", [P, GT, P])
        RG = 6
        x2 = sb("x2", [P, RG, GT, D])
        rows = sb("rows", [P, RR, GT, ROW])
        xn2_hi = sb("xn2_hi", [D, RG, GN], F32R)
        xn2_lo = sb("xn2_lo", [D, RG, GN], F32R)
        biased = sb("biased", [P, GT, E])
        top8 = sb("top8", [P, GT, 8])
        top_index = sb("top_index", [P, GT, 8], U32)
        logits = sb("logits", [P, GT, E])
        tanh_l = sb("tanh_l", [P, GT, E])
        tanh_c = sb("tanh_c", [P, GT, K])
        chosen = sb("chosen", [P, GT, K, E], BF16)
        list_next = sb("list_next", [P, K, E])
        picked = sb("picked", [P, GT, K, E])
        rank = sb("rank", [P, GT, K, E])
        slot_f = sb("slot_f", [P, GT, K])
        slot = sb("slot", [P, RR, GT, K], I32)
        th = sb("th", [P, MC, GN])
        gated = sb("gated", [P, MC, GN])
        hid = sb("hid", [P, 2, MC, GN])
        y_T = sb("y_T", [D, GN])
        acc = sb("acc", [P, 2, GT, D])
        count = sb("count", [P, K, E])
        count_i = sb("count_i", [P, K, E], I32)
        tiles_i = sb("tiles_i", [P, K, E], I32)
        tiles_f = sb("tiles_f", [P, K, E])
        until = sb("until", [P, K, E])
        past = sb("past", [P, K, E])
        past_tiles = sb("past_tiles", [P, K, E])
        expert = sb("expert", [P, K])
        tiles_before = sb("tiles_before", [P, K])
        table = sb("table", [P, 2, K])
        table_row = sb("table_row", [1, 2 * K, P], I32)
        list_end = sb("list_end", [1, K, E], I32)
        NR = 16
        AHEAD = 6
        tile_in = sb("tile_in", [P, NR, ROW])
        TX = 3
        tx_hi = sb("tx_hi", [D, TX, 2, P], F32R)
        tx_lo = sb("tx_lo", [D, TX, 2, P], F32R)
        t_silu = sb("t_silu", [P, 2, M])
        t_hid = sb("t_hid", [P, 2, 2, M])
        th_hi = sb("th_hi", [P, 2, 2 * M], F32R)
        th_lo = sb("th_lo", [P, 2, 2 * M], F32R)
        t_part = sb("t_part", [P, 4, D])
        NO = 8
        t_out = sb("t_out", [P, NO, D])

        gu_pair = [ctx.enter_context(nc.psum_tensor(f"gu_pair{i}", [P, 2, 512], F32)) for i in range(2)]
        banks = [gu_pair[i // 2][:, i % 2] for i in range(4)] + [bank(f"bank{i}")[:, :] for i in range(4, 8)]

        steps = [
            lambda e: e.memset(minus_half[:, :, :], -0.5),
            lambda e: e.memset(ident[:], 0.0),
            lambda e: e.affine_select(out=ident[:], in_=ident[:], compare_op=ALU.not_equal, fill=1.0,
                                      base=0, pattern=[[-1, P]], channel_multiplier=1),
            lambda e: e.tensor_copy(ident_bf[:], ident[:]),
            lambda e: e.memset(ones_bf[:], 1.0),
            lambda e: e.affine_select(out=before_bf[:], in_=ones_bf[:], compare_op=ALU.is_gt, fill=0.0,
                                      base=0, pattern=[[1, P]], channel_multiplier=-1),
            lambda e: e.memset(mask[:], 0.0)]
        for half in range(2):
            part = mask[half * T:(half + 1) * T]
            steps.append(lambda e, part=part: e.affine_select(
                out=part, in_=part, compare_op=ALU.is_ge, fill=MASKED, base=0,
                pattern=[[0, GT], [-1, T]], channel_multiplier=1))
        imprecise = dict(allow_small_or_imprecise_dtypes=True)
        steps += [
            lambda e: e.iota(expert_number[:], pattern=[[1, E]], base=0, channel_multiplier=0, **imprecise),
            lambda e: e.iota(list_start[:], pattern=[[0, K], [LIST, E]], base=0, channel_multiplier=0, **imprecise),
            lambda e: e.iota(tile_number[:], pattern=[[0, 1]], base=0, channel_multiplier=1, **imprecise),
            lambda e: e.memset(ones_e[:], 1.0),
            lambda e: e.memset(choice_start[:, 0:1], 0.0),
            lambda e: e.memset(choice_start[:, 1:2], float(CHOICE)),
            lambda e: e.memset(padding[:], 0.0),
            lambda e: e.memset(padding[:, D:D + 1].bitcast(I32), NO_TOKEN),
            lambda e: e.memset(last_row[:], 0.0),
            lambda e: e.affine_select(out=last_row[:], in_=last_row[:], compare_op=ALU.not_equal, fill=1.0,
                                      base=1 - P, pattern=[[0, P]], channel_multiplier=1)]
        constants = None
        for step in steps:
            constants = do("pool", [constants], step, "const")
        half_ready, ident_ready = ("const", 1), ("const", 3)
        shifted = do("dve", [constants], lambda e: e.tensor_scalar(
            list_start[:, 1], list_start[:, 1], float(CHOICE), None, ALU.add), "list_start")
        shifted = do("dve", [shifted], lambda e: e.tensor_copy(list_next[:, :, :], list_start[:, :, :]), "list_start")

        done = {}

        def at(name, g):
            return done[name, g] if g >= 0 or (name, g) in done else None

        def load_group(g):
            done["x_in", g] = load("sp", [at("x2", g - RX)], x_sb[:, g % RX], x_rows[g], f"x_in{g % RX}")
            done["c_in", g] = load("sp", [at("attended", g - RC)], c_sb[:, g % RC], ctx_rows[g], f"c_in{g % RC}")

        t = do("dve", [], lambda e: e.memset(warm[:], 0.0), "warm")
        zeroed = do("dve", [], lambda e: e.memset(probs_T[:, :, :], 0.0), "zeroed")

        def products(e):
            for _ in range(WARM):
                r = e.matmul(banks[7], warm[:, 0:P], warm[:], start=True, stop=True)
            return r
        warm_up = do("pe", [t], products, "warm_up", ns=WARM * 213)

        load_group(0)
        router_in = load("sp", [], router[:], gate_w, "router_in")
        beta_in = load("sp", [], beta_all[:], beta.rearrange("(a e) -> a e", a=1).broadcast_to([P, E]), "beta_in")
        for g in range(1, LEAD):
            load_group(g)
        for k in range(K):
            done["padding_out", k] = load("act", [constants], sorted_rows[k * CHOICE + E * LIST:(k + 1) * CHOICE, :],
                          padding[:], f"padding_out{k}")
        sources = [(gate_proj[i], up_proj[i], down_proj[i]) for i in range(E)] + [
            (shared_gate[0], shared_up[0], shared_down[0])]

        def load_weights(j, ex):
            b = j % 3
            free = [done.get(("w_lo", j - 3))]
            load("sp", free, staged[:, b, 0:M], sources[ex][0], f"w_in{b}")
            load("sp", free, staged[:, b, M:2 * M], sources[ex][1], f"w_in{b}")
            if ex == E:
                done["w_in", j] = f"w_in{b}", prog.counts[f"w_in{b}"]
                return
            done["w_in", j] = load("sp", free, staged[:, b, 2 * M:].rearrange("p (c h) -> p c h", c=MC),
                                   sources[ex][2].rearrange("(c p) h -> p c h", c=MC), f"w_in{b}")

        def split_weights(j, ex):
            b, w = j % 3, ex * WN

            def parts(v):
                dn = W[:, w + DN_HI:w + WN].rearrange("p (c n h) -> p c n h", c=MC, n=2)
                return {"gu_hi": W[:, w + GU_HI:w + GU_HI + 2 * M], "gu_lo": W[:, w + GU_LO:w + GU_LO + 2 * M],
                        "dn_hi": dn[:, :, 0], "dn_lo": dn[:, :, 1]}[v]
            gu = staged[:, b, 0:2 * M]
            dn = staged[:, b, 2 * M:].rearrange("p (c h) -> p c h", c=MC)

            def hi(e):
                r = e.activation(parts("gu_hi"), gu, ACT.Copy)
                return r if ex == E else e.activation(parts("dn_hi"), dn, ACT.Copy)
            h = do("act", [done["w_in", j]], hi, "w_hi", ns=900)

            def lo(e):
                r = e.tensor_tensor(parts("gu_lo"), gu, parts("gu_hi").bitcast(F32), ALU.subtract)
                return r if ex == E else e.tensor_tensor(parts("dn_lo"), dn, parts("dn_hi").bitcast(F32), ALU.subtract)
            done["w_lo", j] = do("dve", [h], lo, "w_lo", ns=1000 if ex == E else 1700)

        r = do("pe", [router_in, ident_ready],
               lambda e: e.transpose(banks[3][:, 0:E], router[:], ident[0:E, 0:E]), "router_T")
        r = do("dve", [r], lambda e: e.tensor_copy(router_T[:], banks[3][:, 0:E]), "router_T_copy")
        r = do("dve", [r], lambda e: e.tensor_copy(router_parts[:, 0:E], router_T[:]), "router_hi")
        router_done = do("dve", [r], lambda e: e.tensor_tensor(
            router_parts[:, E:2 * E], router_T[:], router_parts[:, 0:E].bitcast(F32), ALU.subtract), "router_lo")

        def moments_of(g, n, slot, src, waits):
            def st(e):
                for i in range(GT):
                    r = e.bn_stats(stats[:, n, i], src[:, i])
                return r
            a = do("dve", waits + [at(f"moments{n}", g - 1)], st, f"stats{n}", ns=820)

            def ag(e):
                for i in range(GT):
                    r = e.bn_aggr(moments[:, slot, n, i], stats[:, n, i])
                return r
            done[f"moments{n}", g] = do("dve", [a, at("shift", (g - LEAD if n == 0 else g) - NS)], ag, f"moments{n}", ns=310)

        def norm_scales(r):
            n0 = 0 if r + LEAD < G else 1
            n1 = 2 if r >= 0 else 1
            s, h = r % NS, slice(n0, n1)
            waits = []
            if n0 == 0:
                waits.append(done["moments0", r + LEAD])
            if n1 == 2:
                waits.append(done["moments1", r])
            free = [at("normal0", r + LEAD - NS), at("normal1", r - NS)]
            c = do("dve", waits + [at("rstd", r - NS)], lambda e: e.tensor_scalar(
                var_eps[:, s, h], moments[:, s, h, :, 1], EPS, None, ALU.add), "var_eps", ns=72)
            done["rstd", r] = c = do("pool", [c, half_ready] + free, lambda e: e.tensor_tensor(
                rstd[:, s, h], var_eps[:, s, h], minus_half[:, h], ALU.pow), "rstd", ns=960)
            done["shift", r] = do("dve", [c] + free, lambda e: e.scalar_tensor_tensor(
                out=shift[:, s, h], in0=moments[:, s, h, :, 0], scalar=-1.0, in1=rstd[:, s, h],
                op0=ALU.mult, op1=ALU.mult), "shift", ns=72)

        def normalise(g, n, dst, src, waits):
            r = g - (LEAD if n == 0 else 0)

            def nm(e):
                for i in range(GT):
                    v = e.activation(dst[:, i], src[:, i], ACT.Identity, bias=shift[:, r % NS, n, i:i + 1],
                                     scale=rstd[:, r % NS, n, i:i + 1])
                return v
            done[f"normal{n}", g] = do("act", [done["shift", r]] + waits, nm, f"normal{n}", ns=1170)

        def query_moments(g):
            moments_of(g, 0, (g - LEAD) % NS, x_sb[:, g % RX], [done["x_in", g]])

        def group_steps(g):
            A, C, O, X, CT = banks[0:5]
            gr, rr = g % RG, g % RR
            normalise(g, 0, xn, x_sb[:, g % RX], [at("xn_transposed", g - 1)])

            def tc(e):
                for i in range(GT):
                    r = e.transpose(CT[:, i * P:(i + 1) * P], c_sb[:, g % RC, i], ident[:])
                return r
            t = do("pe", [done["c_in", g], ident_ready, at("ctx_T", g - 1)], tc, "ctx_transposed", ns=430)
            done["ctx_T", g] = do("act", [t, at("scores", g - 1)], lambda e: e.activation(
                ctx_T[:, :, :], CT[:, :].rearrange("p (b s) -> p b s", b=NB), ACT.Copy), "ctx_T", ns=520)

            def tx(e):
                for i in range(GT):
                    r = e.transpose(A[:, i * P:(i + 1) * P], xn[:, i], ident[:])
                return r
            t = done["xn_transposed", g] = do("pe", [done["normal0", g], at("exp", g - 1)], tx, "xn_transposed", ns=430)
            done["xn_T", g] = do("act", [t, at("scores", g - 1)],
                                 lambda e: e.activation(xn_T[:], A[:], ACT.Copy), "xn_T", ns=520)

            def sc(e):
                e.matmul(A[:, 0:GT * T], ident_bf[:], mask[:, :, :].rearrange("p t k -> p (t k)"),
                         start=True, stop=False, skip_group_check=True)
                for i in range(GT):
                    for half in range(2):
                        q = xn_T[:, i * P + half * T:i * P + (half + 1) * T]
                        r = e.matmul(A[half * T:(half + 1) * T, i * T:(i + 1) * T], q, ctx_T[:, 2 * i + half],
                                     start=False, stop=True, skip_group_check=True)
                return r
            done["scores", g] = do("pe", [done["xn_T", g], done["ctx_T", g], constants], sc, "scores", ns=830)
            S = A[:, 0:GT * T].rearrange("p (t k) -> p t k", t=GT)
            mx = do("dve", [done["scores", g], at("exp_bias", g - 1)],
                    lambda e: e.tensor_reduce(neg_max[:], S, AX_X, ALU.max, negate=True), "row_max", ns=340)
            done["exp_bias", g] = do("dve", [mx, at("exp", g - 1)], lambda e: e.tensor_scalar(
                exp_bias[:], neg_max[:], SCALE, None, ALU.mult), "exp_bias", ns=72)

            def ex(e):
                for i in range(GT):
                    r = e.activation(probs[:, i], S[:, i], ACT.Exp, bias=exp_bias[:, i:i + 1], scale=SCALE,
                                     accum_out=row_sum[:, i:i + 1])
                return r
            done["exp", g] = do("act", [done["exp_bias", g], at("probs_transposed", g - 1), at("inv_sum", g - 1)],
                                ex, "exp", ns=1250)
            done["inv_sum", g] = do("dve", [done["exp", g], at("x2", g - 1)],
                                    lambda e: e.reciprocal(inv_sum[:], row_sum[:]), "inv_sum", ns=95)

            def tp(e):
                for i in range(GT):
                    for half in range(2):
                        h = slice(half * T, (half + 1) * T)
                        r = e.matmul(C[h, i * T:(i + 1) * T], probs[:, i], ident[:, h], start=True, stop=True,
                                     skip_group_check=True)
                return r
            t = done["probs_transposed", g] = do("pe", [done["exp", g], at("probs_T", g - 1)], tp, "probs_transposed", ns=430)
            def pc(e):
                for half in range(2):
                    h = slice(half * T, (half + 1) * T)
                    r = e.activation(probs_T[h, :, h], C[h, 0:GT * T].rearrange("p (t k) -> p t k", t=GT), ACT.Copy)
                return r
            done["probs_T", g] = do("act", [t, zeroed, at("attended", g - 1)], pc, "probs_T", ns=620)

            def pv(e):
                for i in range(GT):
                    r = e.matmul(O[:, i * D:(i + 1) * D], probs_T[:, i], c_sb[:, g % RC, i], start=True, stop=True)
                return r
            done["attended", g] = do("pe", [done["probs_T", g], at("x2", g - 1)], pv, "attended", ns=1280)

            def rs(e):
                for i in range(GT):
                    r = e.scalar_tensor_tensor(out=x2[:, gr, i], in0=O[:, i * D:(i + 1) * D],
                                               scalar=inv_sum[:, i:i + 1], in1=x_sb[:, g % RX, i],
                                               op0=ALU.mult, op1=ALU.add)
                return r
            done["x2", g] = do("dve", [done["attended", g], done["inv_sum", g], at("summed", g - RG)], rs, "x2", ns=1040)
            moments_of(g, 1, g % NS, x2[:, gr], [done["x2", g]])
            if g + LEAD < G:
                query_moments(g + LEAD)
            norm_scales(g)

            sent = [at("scattered0", g - RR), at("scattered1", g - RR)]
            normalise(g, 1, rows[:, rr, :, 0:D], x2[:, gr], sent + [constants])
            done["token_number", g] = do("pool", sent + [constants], lambda e: e.iota(
                rows[:, rr, :, D:D + 1].bitcast(I32), pattern=[[P, GT], [0, 1]], base=g * GN,
                channel_multiplier=1), "token_number", ns=94)

            def tx2(e):
                for i in range(GT):
                    r = e.transpose(X[:, i * P:(i + 1) * P], rows[:, rr, i, 0:D], ident[:])
                return r
            t = do("pe", [done["normal1", g], router_done, at("rank", g - 1), at("list_next", g - 1)],
                   tx2, "xn2_transposed", ns=430)
            hi = do("act", [t, at("up1", g - RG), at("xn2_lo", g - RG)],
                    lambda e: e.activation(xn2_hi[:, gr], X[:], ACT.Copy), "xn2_hi", ns=520)
            done["xn2_lo", g] = do("dve", [hi, at("up1", g - RG)], lambda e: e.tensor_tensor(
                xn2_lo[:, gr], X[:], xn2_hi[:, gr].bitcast(F32), ALU.subtract), "xn2_lo", ns=610)

            def lg(e):
                for i in range(GT):
                    s = slice(i * P, (i + 1) * P)
                    y = X[:, 2 * i * E:2 * (i + 1) * E]
                    e.matmul(y, xn2_hi[:, gr, s], router_parts[:, :], start=True, stop=False, skip_group_check=True)
                    r = e.matmul(y[:, 0:E], xn2_lo[:, gr, s], router_parts[:, 0:E], start=False, stop=True,
                                 skip_group_check=True)
                return r
            t = do("pe", [done["xn2_lo", g]], lg, "logits_mm", ns=860)
            L2 = X[:, 0:GT * 2 * E].rearrange("p (t n e) -> p t n e", t=GT, n=2)
            t = do("dve", [t, at("tanh_logits", g - 1), at("biased", g - 1)], lambda e: e.tensor_reduce(
                logits[:, :, :], L2.rearrange("p t n e -> p t e n"), AX_X, ALU.add), "logits", ns=135)
            L = logits[:, :, :]
            a = done["biased", g] = do("dve", [t, beta_in, at("top_index", g - 1)], lambda e: e.tensor_tensor(
                biased[:, :, :], L,
                beta_all[:, :].rearrange("p (a e) -> p a e", a=1).broadcast_to([P, GT, E]), ALU.add), "biased", ns=102)
            th_l = done["tanh_logits", g] = do("act", [t, a, at("picked", g - 1)], lambda e: e.activation(
                tanh_l[:, :, :], L, ACT.Tanh, scale=0.5), "tanh_logits", ns=200)

            def mx8(e):
                for i in range(GT):
                    r = e.max(top8[:, i], biased[:, i])
                return r
            b = do("dve", [a], mx8, "top8", ns=310)

            def mi(e):
                for i in range(GT):
                    r = e.max_index(top_index[:, i], top8[:, i], biased[:, i])
                return r
            b = done["top_index", g] = do("dve", [b, at("one_hot", g - 1)], mi, "top_index", ns=310)
            hot = done["one_hot", g] = do("dve", [b, constants, at("rank_mm", g - 1), at("list_next", g - 1),
                                                  at("slot", g - 1)], lambda e: e.tensor_tensor(
                chosen[:, :, :, :],
                expert_number[:, :].rearrange("p (a c e) -> p a c e", a=1, c=1).broadcast_to([P, GT, K, E]),
                top_index[:, :, 0:K].rearrange("p t (k a) -> p t k a", a=1).broadcast_to([P, GT, K, E]),
                ALU.is_equal), "one_hot", ns=140)

            def rk(e):
                KE = K * E
                R = X[:, RANKS:RANKS + GT * KE]
                flat = chosen[:, :, :, :].rearrange("p t k e -> p t (k e)")
                e.matmul(R, before_bf[:], flat.rearrange("p t n -> p (t n)"), start=True, stop=False,
                         skip_group_check=True)
                for j in range(GT - 1):
                    e.matmul(R[:, (j + 1) * KE:].rearrange("p (t n) -> p t n", n=KE), ones_bf[:],
                             flat[:, j:j + 1].broadcast_to([P, GT - 1 - j, KE]), start=False, stop=False,
                             skip_group_check=True)
                return e.matmul(R.rearrange("p (t n) -> p t n", n=KE), last_row[:],
                                list_next[:, :, :].rearrange("p (a k) e -> p a (k e)", a=1).broadcast_to([P, GT, KE]),
                                start=False, stop=True, skip_group_check=True)
            done["rank_mm", g] = do("pe", [hot, at("list_next", g - 1), a, th_l, shifted], rk, "rank_mm", ns=450)
            p = done["picked", g] = do("dve", [hot, th_l, at("weights", g - 1)], lambda e: e.tensor_tensor(
                picked[:, :, :, :], chosen[:, :, :, :],
                tanh_l[:, :, :].rearrange("p t (a e) -> p t a e", a=1).broadcast_to([P, GT, K, E]), ALU.mult),
                "picked", ns=135)
            p = do("dve", [p, at("weights", g - 1)], lambda e: e.tensor_reduce(
                tanh_c[:, :, :], picked[:, :, :, :], AX_X, ALU.add), "tanh_chosen", ns=135)
            done["weights", g] = do("dve", [p] + sent, lambda e: e.tensor_scalar(
                rows[:, rr, :, D + 1:D + 1 + K], tanh_c[:, :, :], 0.5, 0.5, ALU.mult, ALU.add), "weights", ns=72)

            R = X[:, RANKS:RANKS + GT * K * E].rearrange("p (t k e) -> p t k e", t=GT, k=K)
            t = done["rank", g] = do("dve", [done["rank_mm", g], at("slot", g - 1)], lambda e: e.tensor_tensor(
                rank[:, :, :, :], chosen[:, :, :, :], R, ALU.mult), "rank", ns=190)
            done["list_next", g] = do("dve", [done["rank_mm", g]], lambda e: e.tensor_tensor(
                list_next[:, :, :], chosen[:, GT - 1], R[:, GT - 1], ALU.add), "list_next", ns=140)
            t = do("dve", [t, at("slot", g - 1)], lambda e: e.tensor_reduce(
                slot_f[:, :, :], rank[:, :, :, :], AX_X, ALU.add), "slot_f", ns=135)
            done["slot", g] = do("dve", [t] + sent, lambda e: e.tensor_copy(slot[:, rr], slot_f[:, :, :]), "slot", ns=75)

            for k in range(K):
                if k == 0 or g < G - DEFER:
                    scatter(g, k, [])

        def scatter(g, k, behind):
            rr = g % RR
            for i in range(GT):
                done[f"scattered{k}", g] = do(
                    "pool", [done["slot", g], done["weights", g], done["normal1", g], done["token_number", g]],
                    lambda e, i=i: e.indirect_dma_start(
                        sorted_rows, bass.IndirectOffsetOnAxis(ap=slot[:, rr, i, k:k + 1], axis=0),
                        rows[:, rr, i, :], None), f"scattered{k}_{rr}", 16, 1040, behind=behind)

        def shared_steps(g, behind):
            G0, U0, G1 = banks[5:8]
            b2, gr = g % 2, g % RG
            for m in range(MC):
                gate, up = ((G0, U0), (G1, G0))[m]
                for k, dst, what in ((0, gate, "gate"), (1, up, "up")):
                    def mm(e, m=m, k=k, dst=dst):
                        c = E * WN + k * M + m * P
                        w = [W[:, c + GU_HI:c + GU_HI + P], W[:, c + GU_LO:c + GU_LO + P]]
                        parts = ((w[0], xn2_hi), (w[0], xn2_lo), (w[1], xn2_hi))
                        for j, (lhs, rhs) in enumerate(parts):
                            r = e.matmul(dst[:], lhs, rhs[:, gr], start=(j == 0), stop=(j == 2))
                        return r
                    free = {"gate0": at("hid1", g - 1), "up0": at("summed", g - 1),
                            "gate1": done["gated1", g - 1] if g else warm_up, "up1": done.get(("gated0", g))}[f"{what}{m}"]
                    done[f"{what}{m}", g] = do("pe", [done["xn2_lo", g], done["w_lo", 0], free], mm,
                                               f"{what}{m}", ns=650, behind=[behind])
                t2 = done[f"tanh{m}", g] = do("act", [done[f"gate{m}", g], at(f"gated{m}", g - 1)], lambda e, m=m, gate=gate:
                    e.activation(th[:, m], gate[:], ACT.Tanh, scale=0.5), f"tanh{m}", ns=480)
                t2 = done[f"gated{m}", g] = do("dve", [t2, at(f"hid{m}", g - 1)], lambda e, m=m, gate=gate:
                    e.scalar_tensor_tensor(out=gated[:, m], in0=th[:, m], scalar=1.0, in1=gate[:],
                                           op0=ALU.add, op1=ALU.mult), f"gated{m}", ns=610)
            for m in range(MC):
                up = (U0, G0)[m]
                done[f"hid{m}", g] = do("dve", [done[f"gated{m}", g], done[f"up{m}", g], at("down", g - 2)],
                                        lambda e, m=m, up=up:
                    e.tensor_tensor(hid[:, g % 2, m], gated[:, m], up[:], ALU.mult), f"hid{m}", ns=610)
            def dn(e):
                for m in range(MC):
                    r = e.matmul(U0[:], shared_dn[:, m], hid[:, g % 2, m], start=(m == 0), stop=(m == MC - 1))
                return r
            t = done["down", g] = do("pe", [done["hid0", g], done["hid1", g], shared_dn_in], dn, "down", ns=1720)
            t = done["y_T", g] = do("act", [t, at("turned", g - 1)],
                                    lambda e: e.activation(y_T[:], U0[:], ACT.Copy, scale=0.5), "y_T", ns=520)

            def tu(e):
                for t in range(GT):
                    r = e.transpose(U0[:, t * P:(t + 1) * P], y_T[:, t * P:(t + 1) * P], ident[:])
                return r
            done["turned", g] = do("pe", [t], tu, "turned", ns=430)
            done["summed", g] = do("dve", [done["turned", g], at("stored", g - 2)], lambda e:
                e.tensor_tensor(acc[:, b2].rearrange("p t d -> p (t d)"), U0,
                                x2[:, gr].rearrange("p t d -> p (t d)"), ALU.add),
                "summed", ns=610)
            done["stored", g] = load("sp", [done["summed", g]], out_rows[g], acc[:, b2], f"stored{b2}")

        load_weights(0, E)
        shared_dn_in = load("sp", [], shared_dn[:, :, :], shared_down[0].rearrange("(c p) h -> p c h", c=MC), "shared_dn_in")
        split_weights(0, E)
        order = [E] + list(range(E))
        for g in range(LEAD):
            query_moments(g)
            norm_scales(g - LEAD)
        BEHIND, GROW = 2, 0.1
        shared_next = 0
        for g in range(G):
            if g + LEAD < G:
                load_group(g + LEAD)
            if 1 <= g <= E:
                load_weights(g, order[g])
                split_weights(g, order[g])
            while shared_next + BEHIND + int(shared_next * GROW) <= g:
                shared_steps(shared_next, at("x2", g - 1))
                shared_next += 1
            group_steps(g)

        last = G - 1
        X = banks[3]
        t = do("pe", [done["list_next", last], done["rank", last], done["slot", last]], lambda e: e.matmul(
            X[:, 0:K * E], last_row[:], list_next[:, :, :].rearrange("p k e -> p (k e)"), start=True, stop=True), "ends")
        ends_mm = X[:, 0:K * E].rearrange("p (k e) -> p k e", k=K)
        ends = do("dve", [t], lambda e: e.tensor_copy(list_end[:, :, :], ends_mm[0:1]), "table")
        t0 = do("dve", [t], lambda e: e.tensor_tensor(count[:, :, :], ends_mm, list_start[:, :, :], ALU.subtract), "table")
        t = do("dve", [t0], lambda e: e.tensor_scalar(count_i[:, :, :], count[:, :, :], float(P - 1), None, ALU.add), "table")
        t = do("dve", [t], lambda e: e.tensor_scalar(tiles_i[:, :, :], count_i[:, :, :], P.bit_length() - 1, None,
                                                     ALU.arith_shift_right), "table")
        t = do("dve", [t], lambda e: e.tensor_copy(tiles_f[:, :, :], tiles_i[:, :, :]), "table")
        for k in range(K):
            t = do("dve", [t], lambda e, k=k: e.tensor_tensor_scan(
                until[:, k], ones_e[:], tiles_f[:, k], 0.0, ALU.mult, ALU.add), "table")
        t = do("dve", [t], lambda e: e.tensor_scalar(past[:, :, :], until[:, :, :], tile_number[:, 0:1], None,
                                                     ALU.is_le), "table")
        u = do("dve", [t], lambda e: e.tensor_reduce(expert[:], past[:, :, :], AX_X, ALU.add), "table")
        t = do("dve", [t], lambda e: e.tensor_tensor(past_tiles[:, :, :], past[:, :, :], tiles_f[:, :, :], ALU.mult), "table")
        t = do("dve", [t], lambda e: e.tensor_reduce(tiles_before[:], past_tiles[:, :, :], AX_X, ALU.add), "table")
        t = do("dve", [t], lambda e: e.tensor_scalar(tiles_before[:], tiles_before[:], tile_number[:, 0:1], -float(P),
                                                     ALU.subtract, ALU.mult), "table")
        t = do("dve", [t, u], lambda e: e.scalar_tensor_tensor(
            out=table[:, 0], in0=expert[:], scalar=float(LIST), in1=tiles_before[:], op0=ALU.mult, op1=ALU.add), "table")
        t = do("dve", [t], lambda e: e.scalar_tensor_tensor(
            out=table[:, 0], in0=table[:, 0], scalar=float(E * LIST), in1=choice_start[:], op0=ALU.min, op1=ALU.add), "table")
        t = do("dve", [t], lambda e: e.tensor_scalar(table[:, 1], expert[:], float(E - 1), float(WN),
                                                     ALU.min, ALU.mult), "table")

        def tr(e):
            for i in range(2 * K):
                r = e.matmul(X[0:1, i * P:(i + 1) * P], table[:, i // K, i % K:i % K + 1], ident[:],
                             start=True, stop=True)
            return r
        t = do("pe", [t, t0, ends], tr, "table_T")
        table_done = do("dve", [t], lambda e: e.tensor_copy(
            table_row[:, :, :].rearrange("p n j -> p (n j)"), X[0:1, 0:2 * K * P]), "table")

        for g in range(shared_next, G):
            shared_steps(g, done["x2", G - 1])
        for g in range(G - DEFER, G):
            scatter(g, 1, [done["scattered0", G - 1]])

        for k in range(K):
            for ex in range(E):
                def pad(e, k=k, ex=ex):
                    v = e.value_load(list_end[0:1, k, ex:ex + 1], min_val=0, max_val=K * CHOICE - P)
                    return e.dma_start(sorted_rows[bass.ds(v, P), :], padding[:])
                padded = do(("sp", "act")[ex % 2], [ends, constants], pad, f"padded{k}{ex % 2}", 16)
                done["padded", k, ex % 2] = padded

        sorted_done = [[done[f"scattered{k}", g] for g in range(G - RR, G)] + [
            done["padded", k, 0], done["padded", k, 1], done["padding_out", k]] for k in range(K)]
        out_written = [done["stored", G - 1], done["stored", G - 2]]
        pairs = K * TILES // 2
        assert K * TILES % 2 == 0
        tok = {}

        def t_at(name, i):
            return tok[name, i] if i >= 0 else None

        def t_load(j):
            k, n = divmod(j, TILES)

            def ld(e):
                v = e.value_load(table_row[0:1, k, n:n + 1], min_val=0, max_val=K * CHOICE - P)
                return e.dma_start(tile_in[:, j % NR], sorted_rows[bass.ds(v, P), :])
            tok["t_in", j] = do("sp", [table_done] + sorted_done[k] + [t_at("t_added", j - NR)], ld, f"t_in{j % NR}", 16, 1060)

        def t_transpose(i):
            def tr(e):
                for h in range(2):
                    r = e.transpose(banks[4][:, h * P:(h + 1) * P], tile_in[:, (2 * i + h) % NR, 0:D], ident[:])
                return r
            first = [done["ctx_T", last]] if i == 0 else []
            t = do("pe", [tok["t_in", 2 * i], tok["t_in", 2 * i + 1], t_at("tx_lo", i - 1)] + first, tr, "t_transposed", ns=215)
            src = banks[4][:, 0:2 * P].rearrange("p (h n) -> p h n", h=2)
            hi = do("act", [t, t_at("t_gate_up", i - TX), t_at("tx_lo", i - TX)],
                    lambda e: e.activation(tx_hi[:, i % TX], src, ACT.Copy), "tx_hi", ns=265)
            tok["tx_lo", i] = do("dve", [hi, t_at("t_gate_up", i - TX)], lambda e: e.tensor_tensor(
                tx_lo[:, i % TX], src, tx_hi[:, i % TX].bitcast(F32), ALU.subtract), "tx_lo", ns=340)

        offsets = {}

        def t_offsets(i):
            def ld(e):
                for h in range(2):
                    k, n = divmod(2 * i + h, TILES)
                    offsets[2 * i + h] = e.value_load(table_row[0:1, K + k, n:n + 1], min_val=0,
                                                      max_val=(E - 1) * WN)
            return ld

        def t_gate_up(i):
            gu = banks[0:2] if i % 2 else banks[2:4]
            earlier = {0: [done["w_lo", E], done["x2", last]], 1: [done["exp", last], done["probs_T", last]]}

            def mm(e):
                if i == 0:
                    t_offsets(0)(e)
                for h in range(2):
                    v = offsets[2 * i + h]
                    w = [W[:, bass.ds(v + GU_HI, 2 * M)], W[:, bass.ds(v + GU_LO, 2 * M)]]
                    for j, (lhs, rhs) in enumerate(((tx_hi, w[0]), (tx_lo, w[0]), (tx_hi, w[1]))):
                        r = e.matmul(gu[h][:], lhs[:, i % TX, h], rhs, start=(j == 0), stop=(j == 2))
                return r
            t = tok["t_gate_up", i] = do("pe", [tok["tx_lo", i], table_done, t_at("t_hid", i - 2)] +
                                         earlier.get(i, []), mm, "t_gate_up", ns=1300,
                                         after=t_offsets(i + 1) if i + 1 < pairs else None)
            g, u = pair_view[i % 2]
            t = do("act", [t, t_at("t_hid", i - 1), done["tanh1", last]], lambda e: e.activation(t_silu[:, :, :], g, ACT.Silu), "t_silu", ns=480)
            tok["t_hid", i] = do("dve", [t, t_at("th_transposed", i - 2)], lambda e: e.tensor_tensor(
                t_hid[:, i % 2], t_silu[:, :, :], u, ALU.mult), "t_hid", ns=610)

        def t_turn(i):
            H = banks[5 + i % 2]

            def tr(e):
                for h in range(2):
                    for m in range(MC):
                        c = (h * MC + m) * P
                        r = e.transpose(H[:, c:c + P], t_hid[:, i % 2, h, m * P:(m + 1) * P], ident[:])
                return r
            t = tok["th_transposed", i] = do(
                "pe", [tok["t_hid", i], t_at("th_lo", i - 2), done["hid1", last], done["summed", last]], tr, "th_transposed", ns=430)
            hi = do("act", [t, t_at("t_down", i - 2), t_at("th_lo", i - 2)],
                    lambda e: e.activation(th_hi[:, i % 2], H[:], ACT.Copy), "th_hi", ns=480)
            tok["th_lo", i] = do("dve", [hi, t_at("t_down", i - 2)], lambda e: e.tensor_tensor(
                th_lo[:, i % 2], H[:], th_hi[:, i % 2].bitcast(F32), ALU.subtract), "th_lo", ns=610)

        def t_down(i):
            Y = banks[7]

            def mm(e):
                for h in range(2):
                    v = offsets.pop(2 * i + h)
                    y = Y[:, h * 2 * D:(h + 1) * 2 * D]
                    for m in range(MC):
                        c = (h * MC + m) * P
                        w = v + (DN_HI + m * 2 * D)
                        e.matmul(y, th_hi[:, i % 2, c:c + P], W[:, bass.ds(w, 2 * D)], start=(m == 0), stop=False,
                                 skip_group_check=True)
                        r = e.matmul(y[:, 0:D], th_lo[:, i % 2, c:c + P], W[:, bass.ds(w, D)], start=False,
                                     stop=(m == MC - 1), skip_group_check=True)
                return r
            t = tok["t_down", i] = do("pe", [tok["th_lo", i], t_at("t_out", i - 1), done["gated1", last]], mm, "t_down", ns=860)
            def half(h):
                n = 2 * i + h
                k = n // TILES
                return n, k, Y[:, h * 2 * D:(h + 1) * 2 * D], tile_in[:, n % NR, D + 1 + k:D + 2 + k]

            for h in range(2):
                n, k, y, weight = half(h)
                part = do("act", [t, t_at("t_out", i - 2)], lambda e, n=n, y=y, weight=weight: e.activation(
                    t_part[:, n % 4], y[:, 0:D], ACT.Copy, scale=weight), "t_part", ns=255)
            for h in range(2):
                n, k, y, weight = half(h)
                a = do("dve", [part, t_at("t_added", n - NO)], lambda e, n=n, y=y, weight=weight: e.scalar_tensor_tensor(
                    out=t_out[:, n % NO], in0=y[:, D:2 * D], scalar=weight, in1=t_part[:, n % 4],
                    op0=ALU.mult, op1=ALU.add), "t_out", ns=200)
                tok["t_out", i] = a
                order = [tok["t_added", q] for q in range(TILES - NR, TILES)] if k else []
                tok["t_added", n] = do("pool", [a] + out_written + order, lambda e, n=n: e.indirect_dma_start(
                    out_flat, bass.IndirectOffsetOnAxis(ap=tile_in[:, n % NR, D:D + 1].bitcast(I32), axis=0),
                    t_out[:, n % NO], None, bounds_check=N - 1, oob_is_err=False, compute_op=ALU.add),
                    f"t_added{n % NR}", 16, 1040)

        pair_view = []
        for b in (gu_pair[1], gu_pair[0]):
            v = b[:, :, :]
            pair_view.append((v[:, :, 0:M], v[:, :, M:2 * M]))
        for j in range(AHEAD):
            t_load(j)
        t_transpose(0)
        t_transpose(1)
        for i in range(pairs + 2):
            if i < pairs:
                for j in (2 * i + AHEAD, 2 * i + AHEAD + 1):
                    if j < 2 * pairs:
                        t_load(j)
                t_gate_up(i)
            if 1 <= i <= pairs:
                t_turn(i - 1)
            if i + 2 < pairs:
                t_transpose(i + 2)
            if i >= 2:
                t_down(i - 2)

        for t in [tok["t_added", q] for q in range(2 * pairs - NR, 2 * pairs)]:
            prog.at_end.append(("pool", t))
        prog.arrange()

        block = ctx.enter_context(nc.Block())

        @block.sync
        def _(e):
            prog.run("sp", e)

        @block.gpsimd
        def _(e):
            prog.run("pool", e)

        @block.scalar
        def _(e):
            prog.run("act", e)

        @block.vector
        def _(e):
            prog.run("dve", e)

        @block.tensor
        def _(e):
            prog.run("pe", e)


_INS = ["x", "ctx_1024", "L0_ffn_gate_w", "L0_ffn_beta", "L0_ffn_gate_proj_w", "L0_ffn_up_proj_w", "L0_ffn_down_proj_w",
        "L0_ffn_shared_gate_w", "L0_ffn_shared_up_w", "L0_ffn_shared_down_w"]


def kernel(**inputs):
    import numpy as np
    import concourse.bacc as bacc
    from concourse.bass_utils import run_bass_kernel_spmd

    nc = bacc.Bacc("TRN2", target_bir_lowering=False, num_devices=1)
    arrays, args = {}, []
    for name in _INS:
        a = np.ascontiguousarray(inputs[name])
        arrays[name] = a
        args.append(nc.dram_tensor(name, a.shape, mybir.dt.from_np(a.dtype), kind="ExternalInput").ap())
    shape = inputs["x"].shape
    args.append(nc.dram_tensor("out", shape, F32, kind="ExternalOutput").ap())
    T, (E, D) = shape[0] * shape[1], inputs["L0_ffn_gate_w"].shape
    args.append(nc.dram_tensor("sorted_rows", (2 * (E * (T + P) + P), D + 3), F32).ap())
    build(nc, *args)
    return run_bass_kernel_spmd(nc, [arrays], core_ids=[0]).results[0]["out"]
```
